# Optimizing a Trainium2 kernel written in Bass

```python
import numpy as np
import jax
import jax.numpy as jnp

def _softmax(x, axis=-1):
    return jax.nn.softmax(x, axis=axis)

def _gelu(x):
    return jax.nn.gelu(x, approximate=True)

def _silu(x):
    return jax.nn.silu(x)

def _sigmoid(x):
    return jax.nn.sigmoid(x)

def _layernorm(x, axis=-1, eps=1e-05):
    m = jnp.mean(x, axis=axis, keepdims=True)
    v = jnp.var(x, axis=axis, keepdims=True)
    return (x - m) / jnp.sqrt(v + eps)

def _scatter_add(tgt, idx, src, axis=0):
    return tgt.at[idx].add(src)

def _segment_sum(src, seg, n):
    return jax.ops.segment_sum(src, seg, n)
kernel_name = 'mk_perceiver_d1_seqx_r4_5c07e9'

def setup_inputs(seed: int=0):
    np.random.seed(seed)
    _w = jnp.asarray

    def _rec_inputs():
        import jax
        import jax.numpy as jnp
        _rk = jax.random.key(seed)
        x = 7.22e-05 + 1 * jax.random.normal(jax.random.fold_in(_rk, 1), (16, 64, 256), jnp.float32)
        _lenS = 64 - jax.random.randint(jax.random.fold_in(_rk, 7), (16,), 0, max(1, 64 // 4) + 1, jnp.int32)
        _lenS2 = 256 - jax.random.randint(jax.random.fold_in(_rk, 8), (16,), 0, max(1, 256 // 4) + 1, jnp.int32)
        _ctx_1024P = jax.random.normal(jax.random.fold_in(_rk, 11), (16, 16, 256), jnp.float32)
        _ctx_1024c = jax.random.dirichlet(jax.random.fold_in(_rk, 511), 0.3 * jnp.ones((16,), jnp.float32), (16, 256))
        _ctx_1024t = jnp.einsum('bsk,bkd->bsd', _ctx_1024c, _ctx_1024P)
        _ctx_1024t = _ctx_1024t * jax.lax.rsqrt(jnp.mean(jnp.square(_ctx_1024t)) + 1e-12) * 0.953939
        ctx_1024 = 4.13588e-05 + 0.999923 * (_ctx_1024t + 0.3 * jax.random.normal(jax.random.fold_in(_rk, 611), (16, 256, 256), jnp.float32))
        return (x, ctx_1024)
    x, ctx_1024 = _rec_inputs()

    def _L0_xattn_setup():
        import jax, jax.numpy as jnp
        import numpy as np
        DMODEL = 256
        DHEAD = 64
        N_HEAD = DMODEL // DHEAD
        key = jax.random.key(seed)
        ks = jax.random.split(key, 6)
        B, L = (4, 512)
        q = jax.random.normal(ks[0], (B, L, DMODEL), dtype=jnp.float32)
        k = jax.random.normal(ks[1], (B, L, DMODEL), dtype=jnp.float32)
        v = jax.random.normal(ks[2], (B, L, DMODEL), dtype=jnp.float32)
        s = 1.0 / np.sqrt(DMODEL)
        Wq = jax.random.normal(ks[3], (DMODEL, DMODEL), dtype=jnp.float32) * s
        Wk = jax.random.normal(ks[4], (DMODEL, DMODEL), dtype=jnp.float32) * s
        Wv = jax.random.normal(ks[5], (DMODEL, DMODEL), dtype=jnp.float32) * s
        return {'q': q, 'k': k, 'v': v, 'Wq': Wq, 'Wk': Wk, 'Wv': Wv}
    _L0_xattn_all = _L0_xattn_setup()
    _L0_xattn_in = {k: v for k, v in _L0_xattn_all.items() if k in ('Wq', 'Wk', 'Wv')}
    del _L0_xattn_all

    def _L0_attn_setup():
        import jax, jax.numpy as jnp
        import numpy as np
        NUM_HEADS = 16
        EPS = 1e-12

        def _l2norm(t):
            n = jnp.sqrt(jnp.sum(t * t, axis=-1, keepdims=True))
            return t / jnp.maximum(n, EPS)
        key = jax.random.key(seed)
        kx, kq, kk, kv = jax.random.split(key, 4)
        B, S, E = (2, 512, 256)
        head_dim = E // NUM_HEADS
        bound = 1.0 / np.sqrt(E)
        x = jax.random.normal(kx, (B, S, E), dtype=jnp.float32)
        Wq = jax.random.uniform(kq, (E, E), dtype=jnp.float32, minval=-bound, maxval=bound)
        Wk = jax.random.uniform(kk, (E, E), dtype=jnp.float32, minval=-bound, maxval=bound)
        Wv = jax.random.uniform(kv, (E, E), dtype=jnp.float32, minval=-bound, maxval=bound)
        g_scale = jnp.asarray(np.sqrt(head_dim), dtype=jnp.float32)
        return {'x': x, 'Wq': Wq, 'Wk': Wk, 'Wv': Wv, 'g_scale': g_scale}
    _L0_attn_all = _L0_attn_setup()
    _L0_attn_in = {k: v for k, v in _L0_attn_all.items() if k in ('Wq', 'Wk', 'Wv', 'g_scale')}
    del _L0_attn_all

    def _L0_ffn_setup():
        import jax, jax.numpy as jnp
        import numpy as np
        H = 256
        I = 128
        E = 8
        K = 2
        SI = I * 2
        B, S = (2, 256)

        def _mlp(x, gw, uw, dw):
            return jax.nn.silu(x @ gw.T) * (x @ uw.T) @ dw.T
        key = jax.random.key(seed)
        ks = jax.random.split(key, 9)
        s = 0.02
        return {'x': jax.random.normal(ks[0], (B, S, H), jnp.float32), 'gate_w': jax.random.normal(ks[1], (E, H), jnp.float32) * s, 'lb_bias': jnp.zeros((E,), jnp.float32), 'expert_gate_w': jax.random.normal(ks[2], (E, I, H), jnp.float32) * s, 'expert_up_w': jax.random.normal(ks[3], (E, I, H), jnp.float32) * s, 'expert_down_w': jax.random.normal(ks[4], (E, H, I), jnp.float32) * s, 'shared_gate_w': jax.random.normal(ks[5], (SI, H), jnp.float32) * s, 'shared_up_w': jax.random.normal(ks[6], (SI, H), jnp.float32) * s, 'shared_down_w': jax.random.normal(ks[7], (H, SI), jnp.float32) * s}
    _L0_ffn_all = _L0_ffn_setup()
    _L0_ffn_in = {k: v for k, v in _L0_ffn_all.items() if k in ('gate_w', 'lb_bias', 'expert_gate_w', 'expert_up_w', 'expert_down_w', 'shared_gate_w', 'shared_up_w', 'shared_down_w')}
    del _L0_ffn_all
    return {'x': x, 'ctx_1024': ctx_1024, 'L0_xattn_Wq': _L0_xattn_in['Wq'], 'L0_xattn_Wk': _L0_xattn_in['Wk'], 'L0_xattn_Wv': _L0_xattn_in['Wv'], 'L0_attn_Wq': _L0_attn_in['Wq'], 'L0_attn_Wk': _L0_attn_in['Wk'], 'L0_attn_Wv': _L0_attn_in['Wv'], 'L0_attn_g_scale': _L0_attn_in['g_scale'], 'L0_ffn_gate_w': _L0_ffn_in['gate_w'], 'L0_ffn_lb_bias': _L0_ffn_in['lb_bias'], 'L0_ffn_expert_gate_w': _L0_ffn_in['expert_gate_w'], 'L0_ffn_expert_up_w': _L0_ffn_in['expert_up_w'], 'L0_ffn_expert_down_w': _L0_ffn_in['expert_down_w'], 'L0_ffn_shared_gate_w': _L0_ffn_in['shared_gate_w'], 'L0_ffn_shared_up_w': _L0_ffn_in['shared_up_w'], 'L0_ffn_shared_down_w': _L0_ffn_in['shared_down_w']}

def reference(x, ctx_1024, L0_xattn_Wq, L0_xattn_Wk, L0_xattn_Wv, L0_attn_Wq, L0_attn_Wk, L0_attn_Wv, L0_attn_g_scale, L0_ffn_gate_w, L0_ffn_lb_bias, L0_ffn_expert_gate_w, L0_ffn_expert_up_w, L0_ffn_expert_down_w, L0_ffn_shared_gate_w, L0_ffn_shared_up_w, L0_ffn_shared_down_w):
    import jax
    import jax.numpy as jnp

    def _L0_xattn_ref(q, k, v, Wq, Wk, Wv):
        import jax, jax.numpy as jnp
        import numpy as np
        DMODEL = 256
        DHEAD = 64
        N_HEAD = DMODEL // DHEAD
        b, lq, _ = q.shape
        lv = v.shape[1]
        qh = (q @ Wq.T).reshape(b, lq, N_HEAD, DHEAD).transpose(0, 2, 1, 3)
        kh = (k @ Wk.T).reshape(b, lv, N_HEAD, DHEAD).transpose(0, 2, 1, 3)
        vh = (v @ Wv.T).reshape(b, lv, N_HEAD, DHEAD).transpose(0, 2, 1, 3)
        scale = 1.0 / jnp.sqrt(jnp.asarray(DHEAD, dtype=qh.dtype))
        scores = jnp.einsum('bhqd,bhkd->bhqk', qh, kh) * scale
        attn = jax.nn.softmax(scores, axis=-1)
        out = jnp.einsum('bhqk,bhkd->bhqd', attn, vh)
        return out.transpose(0, 2, 1, 3).reshape(b, lq, DMODEL)

    def _L0_attn_ref(x, Wq, Wk, Wv, g_scale):
        import jax, jax.numpy as jnp
        import numpy as np
        NUM_HEADS = 16
        EPS = 1e-12

        def _l2norm(t):
            n = jnp.sqrt(jnp.sum(t * t, axis=-1, keepdims=True))
            return t / jnp.maximum(n, EPS)
        B, S, E = x.shape
        H = NUM_HEADS
        D = E // H
        q = (x @ Wq.T).reshape(B, S, H, D).transpose(0, 2, 1, 3)
        k = (x @ Wk.T).reshape(B, S, H, D).transpose(0, 2, 1, 3)
        v = (x @ Wv.T).reshape(B, S, H, D).transpose(0, 2, 1, 3)
        q = _l2norm(q)
        k = _l2norm(k)
        scores = g_scale * jnp.einsum('bhqd,bhkd->bhqk', q, k)
        attn = jax.nn.softmax(scores, axis=-1)
        out = jnp.einsum('bhqk,bhkd->bhqd', attn, v)
        out = out.transpose(0, 2, 1, 3).reshape(B, S, E)
        return out

    def _L0_ffn_ref(x, gate_w, lb_bias, expert_gate_w, expert_up_w, expert_down_w, shared_gate_w, shared_up_w, shared_down_w):
        import jax, jax.numpy as jnp
        import numpy as np
        H = 256
        I = 128
        E = 8
        K = 2
        SI = I * 2
        B, S = (2, 256)

        def _mlp(x, gw, uw, dw):
            return jax.nn.silu(x @ gw.T) * (x @ uw.T) @ dw.T
        b, s, h = x.shape
        xf = x.reshape(-1, h)
        logits = xf @ gate_w.T + lb_bias
        scores = jax.nn.sigmoid(logits.astype(jnp.float32))
        topw, topi = jax.lax.top_k(scores, K)
        topw = (topw / (topw.sum(-1, keepdims=True) + 1e-08)).astype(x.dtype)
        out = jnp.zeros_like(xf)
        for e in range(E):
            m = topi == e
            sel = m.any(axis=-1)
            cnt = m.sum()
            wmean = (topw * m).sum() / jnp.maximum(cnt, 1).astype(topw.dtype)
            y = _mlp(xf, expert_gate_w[e], expert_up_w[e], expert_down_w[e])
            out = out + jnp.where(sel[:, None], y * wmean, jnp.zeros((), x.dtype))
        out = out.reshape(b, s, h)
        out = out + _mlp(x, shared_gate_w, shared_up_w, shared_down_w)
        return out
    x = x + _L0_xattn_ref(_layernorm(x, axis=-1), ctx_1024, ctx_1024, L0_xattn_Wq, L0_xattn_Wk, L0_xattn_Wv)
    x = x + _L0_attn_ref(_layernorm(x, axis=-1), L0_attn_Wq, L0_attn_Wk, L0_attn_Wv, L0_attn_g_scale)
    x = x + _L0_ffn_ref(_layernorm(x, axis=-1), L0_ffn_gate_w, L0_ffn_lb_bias, L0_ffn_expert_gate_w, L0_ffn_expert_up_w, L0_ffn_expert_down_w, L0_ffn_shared_gate_w, L0_ffn_shared_up_w, L0_ffn_shared_down_w)
    return x

_drawn_inputs = setup_inputs


def setup_inputs(seed=0):
    import zlib

    import numpy as np

    out = dict(_drawn_inputs(seed))
    spreads = {'L0_ffn_lb_bias': (0.0, 0.8)}
    factors = {'L0_ffn_gate_w': 8.0,
     'L0_ffn_expert_gate_w': 7.964,
     'L0_ffn_expert_up_w': 7.842,
     'L0_ffn_expert_down_w': 7.798,
     'L0_ffn_shared_gate_w': 3.946,
     'L0_ffn_shared_up_w': 3.883,
     'L0_ffn_shared_down_w': 3.911}
    for name, (base, spread) in spreads.items():
        noise = np.random.default_rng([zlib.crc32(name.encode()), seed]).standard_normal(out[name].shape)
        drawn = base * np.exp(spread * noise) if base else spread * noise
        out[name] = jnp.asarray(drawn.astype(out[name].dtype))
    for name, factor in factors.items():
        out[name] = (out[name] * factor).astype(out[name].dtype)
    return out
```

```python
from contextlib import ExitStack

import concourse.bass as bass
from concourse import mybir

ALU = mybir.AluOpType
ACT = mybir.ActivationFunctionType
AX = mybir.AxisListType
F32 = mybir.dt.float32
F32R = mybir.dt.float32r
F16 = mybir.dt.float16

P = 128
D = 256
KC = D // P
BATCH = 16
SEQ = 64
CTX = 256
TOK = BATCH * SEQ
TILES = TOK // P
GB = P // SEQ
GK = GB * CTX
XH = 4
XD = D // XH
XP = XH // 2
SH = 16
SD = D // SH
SP_ = SH // 2
NE = 8
CH = 128
SHARED = 2
CHUNKS = SHARED + NE
WC = 2 * KC * CH + D
HALF = TOK // 2
EPS_LN = 1e-5
EPS_NORM = 1e-12
XSCALE = float(XD) ** -0.5
LIFT = 8.317766166719343

PARTS = ((0, 0), (0, 1), (1, 0))


def build(nc, x, ctx_t, w_cross, w_self, g_scale, gate_w, lb_bias, w_ffn, ident32, ident16, rank, out):
    with ExitStack() as ctx:
        def sb(name, shape, dt=F32):
            return ctx.enter_context(nc.sbuf_tensor(name, shape, dt))

        def sem(name):
            return ctx.enter_context(nc.semaphore(name))

        id32 = sb("id32", [P, P])
        id16 = sb("id16", [P, P], F16)
        rank_sb = sb("rank_sb", [P, TILES, NE])
        ones = sb("ones", [P, P])
        minus_half = sb("minus_half", [P, 2 * SH])
        g_sb = sb("g_sb", [P, 1])
        g_shift = sb("g_shift", [P, 1])
        bias_sb = sb("bias_sb", [NE, 1])
        bias_neg = sb("bias_neg", [NE, 1])
        gate_raw = sb("gate_raw", [P, KC, NE])
        gate_hl = [sb(f"gate_{n}", [P, KC, P], F32R) for n in ("hi", "lo")]
        xs = sb("xs", [P, TILES, D])
        wx_raw = sb("wx_raw", [P, 3, KC, D])
        wx = [sb(f"wx_{n}", [P, 3, KC, D], F32R) for n in ("hi", "lo")]
        ws_raw = sb("ws_raw", [P, KC, 3 * D])
        ws = [sb(f"ws_{n}", [P, KC, 3 * D], F32R) for n in ("hi", "lo")]
        stats = [sb(f"stats{n}", [P, TILES, 6]) for n in range(3)]
        meanvar = [sb(f"meanvar{n}", [P, TILES, 2]) for n in range(3)]
        veps = [sb(f"veps{n}", [P, TILES]) for n in range(3)]
        rstd = [sb(f"rstd{n}", [P, TILES]) for n in range(3)]
        xn1 = sb("xn1", [P, 2, D])
        xn2 = sb("xn2", [P, D])
        xn3 = sb("xn3", [P, D])
        lnt = [sb(f"lnt_{n}", [P, KC, TOK], F32R) for n in ("hi", "lo")]
        ln2t = [sb(f"ln2t_{n}", [P, KC, P], F32R) for n in ("hi", "lo")]
        ctx_raw = [sb(f"ctx_raw{n}", [P, KC, GK]) for n in range(2)]
        cx = [sb(f"cx_{n}", [P, 2, KC, GK], F32R) for n in ("hi", "lo")]
        qbd = [sb(f"qbd_{n}", [P, XP, BATCH, P], F32R) for n in ("hi", "lo")]
        kt = [sb(f"kt_{n}", [P, XP, GK], F32R) for n in ("hi", "lo")]
        vx = [sb(f"vx_{n}", [P, 2, GK // P, XH, XD + 1], F16) for n in ("hi", "lo")]
        negmax = sb("negmax", [P, TILES, GB, XP])
        p32 = sb("p32", [P, GB, XP, CTX])
        ph = [sb(f"p_{n}", [P, GB, XP, CTX], F16) for n in ("hi", "lo")]
        pt = sb("pt", [P, GB, 2, KC, XH, SEQ], F16)
        rsum = sb("rsum", [P, TILES, XH])
        att = sb("att", [P, D])
        raw = sb("raw", [P, 2 * D])
        sq = sb("sq", [P, 2 * D])
        ss = sb("ss", [P, 2 * SH])
        ssm = sb("ssm", [P, 2 * SH])
        rnorm = sb("rnorm", [P, 2, 2 * SH])
        unit = sb("unit", [P, 2, SH, SD])
        stack = [sb(f"stack_{n}", [P, SH, 4, SD], F16) for n in ("q", "k")]
        qt = sb("qt", [P, SP_, P], F16)
        kbd = sb("kbd", [P, SP_, GB, 2, SEQ], F16)
        vbd = [sb(f"vbd_{n}", [P, 3, GB, SP_, 2, SD + 1], F16) for n in ("hi", "lo")]
        s32 = sb("s32", [P, GB, SP_, SEQ])
        sh = [sb(f"s_{n}", [P, GB, SP_, SEQ], F16) for n in ("hi", "lo")]
        rsum2 = sb("rsum2", [P, TILES, SH])
        att2 = sb("att2", [P, D])
        et = sb("et", [NE, TOK])
        S = sb("S", [P, TILES, NE])
        r1 = sb("r1", [P, TILES, NE])
        onehot = [sb(f"onehot{n}", [P, TILES, NE]) for n in range(2)]
        rest = sb("rest", [P, TILES, NE])
        top = [sb(f"top{n}", [P, TILES]) for n in range(2)]
        pick = sb("pick", [P, TILES])
        den = sb("den", [P, TILES])
        rden = sb("rden", [P, TILES])
        tally = sb("tally", [P, TILES, 2, NE])
        total = sb("total", [P, 2 * NE])
        cnt = sb("cnt", [P, NE])
        rcnt = sb("rcnt", [P, NE])
        wmean = sb("wmean", [P, NE])
        coef = sb("coef", [P, TILES, NE])
        wf_raw = [wx_raw[:, :, :, :].rearrange("p a c n -> p (a c n)")[:, n * WC:(n + 1) * WC] for n in range(2)]
        wf = [sb(f"wf_{n}", [P, 2, WC], F32R) for n in ("hi", "lo")]
        sg = p32[:, :, :, :].rearrange("p b m k -> p b (m k)")
        h32 = s32[:, :, :, :].rearrange("p b a q -> p b (a q)")
        hh = [qbd[n][:, :, :, :].rearrange("p m b q -> p (m b q)")[:, 0:2 * TOK].rearrange("p (u t) -> p u t", u=2)
              for n in range(2)]

        ps = ctx.enter_context(nc.psum_tensor("ps", [P, 8, 512], F32))

        def bank(b):
            return ps[:, b, :]

        d_const = sem("d_const")
        d_x = [sem(f"d_x{n}") for n in range(2)]
        d_wx, d_ws = sem("d_wx"), sem("d_ws")
        d_ctx = [sem(f"d_ctx{n}") for n in range(2)]
        d_wf = [sem(f"d_wf{n}") for n in range(2)]
        d_out = sem("d_out")
        zeroed = sem("zeroed")
        pool_veps = sem("pool_veps")
        rstd_ready = [sem(f"rstd{n}_ready") for n in range(3)]
        wx_hi, wx_lo = sem("wx_hi"), sem("wx_lo")
        ws_hi, ws_lo = sem("ws_hi"), sem("ws_lo")
        cx_hi, cx_lo = sem("cx_hi"), sem("cx_lo")
        wf_hi, wf_lo = sem("wf_hi"), sem("wf_lo")
        p_lo, s_lo, p_hi, s_hi = sem("p_lo"), sem("s_lo"), sem("p_hi"), sem("s_hi")
        rnorm_ready = sem("rnorm_ready")
        ln1_turned = sem("ln1_turned")
        q_done = sem("q_done")
        s_done, ss_done = sem("s_done"), sem("ss_done")
        k_done, v_done = sem("k_done"), sem("v_done")
        ln2_turned, ln3_turned = sem("ln2_turned"), sem("ln3_turned")
        p_turned, pv_done, spv_done = sem("p_turned"), sem("pv_done"), sem("spv_done")
        qkv_done = sem("qkv_done")
        q_turned, k_turned = sem("q_turned"), sem("k_turned")
        logits_done, e_turned, tally_done = sem("logits_done"), sem("e_turned"), sem("tally_done")
        gate_done, up_done, down_done = sem("gate_done"), sem("up_done"), sem("down_done")
        ln1_hi, q_hi = sem("ln1_hi"), sem("q_hi")
        exp_done, sexp_done = sem("exp_done"), sem("sexp_done")
        ln2_hi, ln3_hi = sem("ln2_hi"), sem("ln3_hi")
        k_hi, v_hi, pt_ready = sem("k_hi"), sem("v_hi"), sem("pt_ready")
        raw_ready, sq_ready, sv_hi = sem("raw_ready"), sem("sq_ready"), sem("sv_hi")
        kbd_ready, et_ready = sem("kbd_ready"), sem("et_ready")
        sg_ready, h_hi = sem("sg_ready"), sem("h_hi")
        const_ready = sem("const_ready")
        stat_ready = sem("stat_ready")
        ln_stats = [sem(f"ln{n}_stats") for n in range(3)]
        xn1_ready, xn2_ready, xn3_ready = sem("xn1_ready"), sem("xn2_ready"), sem("xn3_ready")
        ln1_lo, q_lo = sem("ln1_lo"), sem("q_lo")
        negmax_ready = sem("negmax_ready")
        unit_ready, stack_hi, stack_ready = sem("unit_ready"), sem("stack_hi"), sem("stack_ready")
        ln2_lo, ln3_lo = sem("ln2_lo"), sem("ln3_lo")
        k_lo, v_lo, sv_lo = sem("k_lo"), sem("v_lo"), sem("sv_lo")
        ss_sum, ss_ready = sem("ss_sum"), sem("ss_ready")
        rsum_ready, att_ready, x_cross = sem("rsum_ready"), sem("att_ready"), sem("x_cross")
        rsum2_ready, att2_ready, x_self = sem("rsum2_ready"), sem("att2_ready"), sem("x_self")
        qt_ready = sem("qt_ready")
        route = sem("route")
        tally_ready, coef_ready = sem("tally_ready"), sem("coef_ready")
        h_ready, h_lo, x_ffn = sem("h_ready"), sem("h_lo"), sem("x_ffn")

        SLOTS = TILES + 5

        def tile_of(slot, lag):
            g = slot - lag
            return g if 0 <= g < TILES else None

        block = ctx.enter_context(nc.Block())

        @block.sync
        def _(sp):
            for dst, src in ((id32[:, :], ident32), (id16[:, :], ident16), (rank_sb[:, :, :], rank),
                             (g_sb[:, :], g_scale), (bias_sb[:, :], lb_bias), (gate_raw[:, :, :], gate_w)):
                sp.dma_start(dst, src).then_inc(d_const, 16)
            for n in range(2):
                h = TILES // 2
                sp.dma_start(xs[:, n * h:(n + 1) * h, :],
                             x.rearrange("(t p) d -> p t d", p=P)[:, n * h:(n + 1) * h, :]).then_inc(d_x[n], 16)
            sp.dma_start(wx_raw[:, :, :, :], w_cross).then_inc(d_wx, 16)
            for g in range(TILES):
                if g == 2:
                    sp.dma_start(ws_raw[:, :, :], w_self).then_inc(d_ws, 16)
                if g >= 2:
                    sp.wait_ge(cx_lo, g - 1)
                sp.dma_start(ctx_raw[g % 2][:, :, :], ctx_t[g]).then_inc(d_ctx[g % 2], 16)
            for c in range(CHUNKS):
                if c == 0:
                    sp.wait_ge(wx_lo, 3)
                if c >= 2:
                    sp.wait_ge(wf_lo, c - 1)
                sp.dma_start(wf_raw[c % 2], w_ffn[c]).then_inc(d_wf[c % 2], 16)
            for n in range(TILES // 2):
                sp.wait_ge(x_ffn, (CHUNKS - 1) * TILES + 2 * n + 2)
                sp.dma_start(out.rearrange("(t p) d -> p t d", p=P)[:, 2 * n:2 * n + 2, :],
                             xs[:, 2 * n:2 * n + 2, :]).then_inc(d_out, 16)
            sp.wait_ge(d_out, 16 * (TILES // 2))

        @block.gpsimd
        def _(pool):
            def split_hi(dst, src):
                return pool.tensor_scalar(dst, src, 1.0, 0.0, ALU.mult, ALU.add)

            for n in range(2):
                pool.memset(qbd[n][:, :, :, :].bitcast(F32), 0.0).then_inc(zeroed, 1)
                pool.memset(gate_hl[n][:, :, :].bitcast(F32), 0.0).then_inc(zeroed, 1)
            pool.memset(kbd[:, :, :, :, :], 0.0).then_inc(zeroed, 1)
            pool.memset(vbd[1][:, :, :, :, :, :], 0.0).then_inc(zeroed, 1)
            pool.memset(vbd[0][:, :, :, :, :, :], 0.0).then_inc(zeroed, 1)
            pool.memset(vx[1][:, :, :, :, XD:], 0.0).then_inc(zeroed, 1)
            pool.memset(vx[0][:, :, :, :, XD:], 1.0).then_inc(zeroed, 1)
            pool.wait_ge(zeroed, 9)
            for j in range(2):
                rows = slice(j * SEQ, (j + 1) * SEQ)
                pool.memset(vbd[0][rows, :, :, :, j, SD:], 1.0).then_inc(zeroed, 1)
                pool.wait_ge(zeroed, 10 + j)

            def inverse_std(n, g0, g1, stats_done):
                pool.wait_ge(ln_stats[n], stats_done)
                pool.tensor_scalar(veps[n][:, g0:g1], meanvar[n][:, g0:g1, 1], 1.0, EPS_LN, ALU.mult, ALU.add
                                   ).then_inc(pool_veps, 1)
                count["veps"] += 1
                pool.wait_ge(pool_veps, count["veps"])
                pool.tensor_tensor(rstd[n][:, g0:g1], veps[n][:, g0:g1], minus_half[:, 0:g1 - g0], ALU.pow
                                   ).then_inc(rstd_ready[n], g1 - g0)

            count = {"veps": 0}

            def context_hi(g):
                pool.wait_ge(d_ctx[g % 2], 16 * (g // 2 + 1))
                if g >= 2:
                    pool.wait_ge(v_done, (GK // P) * (g - 1))
                split_hi(cx[0][:, g % 2], ctx_raw[g % 2][:, :, :]).then_inc(cx_hi, 1)

            def chunk_hi(c):
                pool.wait_ge(d_wf[c % 2], 16 * (c // 2 + 1))
                if c >= 2:
                    pool.wait_ge(down_done, TILES * (c - 1))
                split_hi(wf[0][:, c % 2, :], wf_raw[c % 2]).then_inc(wf_hi, 1)

            pool.wait_ge(const_ready, 2)
            context_hi(0)
            inverse_std(0, 0, TILES // 2, TILES // 2)
            inverse_std(0, TILES // 2, TILES, TILES)
            pool.wait_ge(d_ws, 16)
            split_hi(ws[0][:, :, :], ws_raw[:, :, :]).then_inc(ws_hi, 1)

            for i in range(SLOTS):
                g = tile_of(i, 1)
                if g is not None:
                    for b in range(GB):
                        pool.wait_ge(p_hi, GB * g + b + 1)
                        if g >= 1:
                            pool.wait_ge(p_turned, GB * g)
                        pool.tensor_tensor(ph[1][:, b], p32[:, b], ph[0][:, b], ALU.subtract).then_inc(p_lo, 1)
                g = tile_of(i, 4)
                if g is not None:
                    for b in range(GB):
                        pool.wait_ge(s_hi, GB * g + b + 1)
                        if g >= 1:
                            pool.wait_ge(spv_done, g)
                        pool.tensor_tensor(sh[1][:, b], s32[:, b], sh[0][:, b], ALU.subtract).then_inc(s_lo, 1)
                if i + 1 < TILES:
                    context_hi(i + 1)
                g = tile_of(i, 2)
                if g is not None:
                    pool.wait_ge(ss_ready, g + 1)
                    if g >= 2:
                        pool.wait_ge(unit_ready, g - 1)
                    pool.tensor_tensor(rnorm[:, g % 2, :], ssm[:, :], minus_half[:, :], ALU.pow
                                       ).then_inc(rnorm_ready, 1)
                g = tile_of(i, 1)
                if g is not None:
                    inverse_std(1, g, g + 1, g + 1)
                g = tile_of(i, 4)
                if g is not None:
                    inverse_std(2, g, g + 1, g + 1)
                if i in (SLOTS - 3, SLOTS - 2):
                    chunk_hi(i - (SLOTS - 3))
            for c in range(2, CHUNKS):
                chunk_hi(c)

        @block.scalar
        def _(act):
            act.wait_ge(d_wx, 16)
            for n in range(3):
                act.copy(wx[0][:, n], wx_raw[:, n]).then_inc(wx_hi, 1)
            for n in range(TILES // 2):
                act.wait_ge(ln1_turned, 2 * (n + 1))
                act.copy(lnt[0][:, :, n * 2 * P:(n + 1) * 2 * P].rearrange("p c (t m) -> p t c m", t=2),
                         bank(4 + n).rearrange("p (t c m) -> p t c m", t=2, c=KC)).then_inc(ln1_hi, 1)
            act.wait_ge(zeroed, 11)
            for half in range(2):
                for m in range(XP):
                    act.wait_ge(q_done, 2 * half + m + 1)
                    src = bank(2 * half + m).rearrange("p (b q) -> p b q", q=SEQ)
                    for j in range(2):
                        rows = slice(j * XD, (j + 1) * XD)
                        act.activation(qbd[0][rows, m, half * 8:half * 8 + 8, j * SEQ:(j + 1) * SEQ], src[rows],
                                       ACT.Copy, scale=XSCALE).then_inc(q_hi, 1)

            for i in range(SLOTS):
                g = tile_of(i, 1)
                if g is not None:
                    for b in range(GB):
                        act.wait_ge(negmax_ready, GB * g + b + 1)
                        if g >= 1:
                            act.wait_ge(p_lo, GB * (g - 1) + b + 1)
                        for m in range(XP):
                            ins = act.activation(p32[:, b, m], bank(4 + b)[:, m * CTX:(m + 1) * CTX], ACT.Exp,
                                                 bias=negmax[:, g, b, m:m + 1])
                        ins.then_inc(exp_done, 1)
                g = tile_of(i, 4)
                if g is not None:
                    for b in range(GB):
                        act.wait_ge(ss_done, GB * g + b + 1)
                        if g >= 1:
                            act.wait_ge(s_lo, GB * (g - 1) + b + 1)
                        act.activation(s32[:, b], bank(6 + b).rearrange("p (a q) -> p a q", q=SEQ), ACT.Exp,
                                       bias=g_shift[:, 0:1], scale=g_sb[:, 0:1]).then_inc(sexp_done, 1)
                g = tile_of(i, 2)
                if g is not None:
                    act.wait_ge(ln2_turned, g + 1)
                    act.copy(ln2t[0][:, :, :], bank(2)[:, 0:D].rearrange("p (c m) -> p c m", c=KC)
                             ).then_inc(ln2_hi, 1)
                g = tile_of(i, 5)
                if g is not None:
                    act.wait_ge(ln3_turned, g + 1)
                    act.copy(lnt[0][:, :, g * P:(g + 1) * P], bank(3)[:, 0:D].rearrange("p (c m) -> p c m", c=KC)
                             ).then_inc(ln3_hi, 1)
                g = tile_of(i, 0)
                if g is not None:
                    for m in range(XP):
                        act.wait_ge(k_done, XP * g + m + 1)
                        act.copy(kt[0][:, m, :], bank(m)).then_inc(k_hi, 1)
                g = tile_of(i, 1)
                if g is not None:
                    for b in range(GB):
                        act.wait_ge(p_turned, GB * g + b + 1)
                        act.copy(pt[:, b].rearrange("p s c h q -> p (s c h q)"), bank(4 + b).bitcast(F16)
                                 ).then_inc(pt_ready, 1)
                g = tile_of(i, 0)
                if g is not None:
                    for n in range(2):
                        act.wait_ge(v_done, (GK // P) * g + 2 * n + 2)
                        act.copy(vx[0][:, g % 2, 2 * n:2 * n + 2, :, 0:XD],
                                 bank(3 - n).rearrange("p (t h d) -> p t h d", t=2, h=XH)).then_inc(v_hi, 1)
                g = tile_of(i, 2)
                if g is not None:
                    act.wait_ge(qkv_done, 2 * g + 1)
                    if g >= 1:
                        act.wait_ge(unit_ready, g)
                        act.wait_ge(ss_sum, g)
                    act.copy(raw[:, :], bank(0)).then_inc(raw_ready, 1)
                    act.activation(sq[:, :], bank(0), ACT.Square).then_inc(sq_ready, 1)
                    act.wait_ge(qkv_done, 2 * g + 2)
                    for b in range(GB):
                        for j in range(2):
                            src = bank(1)[b * SEQ:(b + 1) * SEQ, 0:D].rearrange("p (a j d) -> p a j d", j=2, d=SD)
                            act.copy(vbd[0][j * SEQ:(j + 1) * SEQ, g % 3, b, :, j, 0:SD], src[:, :, j]
                                     ).then_inc(sv_hi, 1)
                g = tile_of(i, 3)
                if g is not None:
                    act.wait_ge(k_turned, g + 1)
                    src = bank(5).bitcast(F16).rearrange("p (a b k) -> p a b k", a=SP_, b=GB)
                    for j in range(2):
                        rows = slice(j * 4 * SD, (j + 1) * 4 * SD)
                        act.copy(kbd[rows, :, :, j, :], src[rows]).then_inc(kbd_ready, 1)

            for n in range(2):
                act.wait_ge(logits_done, n + 1)
                act.activation(et[:, n * HALF:(n + 1) * HALF], bank(4 + n)[0:NE, :], ACT.Exp,
                               bias=bias_neg[:, 0:1], scale=-1.0).then_inc(et_ready, 1)
            act.wait_ge(p_lo, GB * TILES)
            act.wait_ge(s_done, GB * TILES)
            for c in range(CHUNKS):
                for n in range(2):
                    act.wait_ge(gate_done, 2 * c + n + 1)
                    if c >= 1:
                        act.wait_ge(h_ready, 2 * (c - 1) + n + 1)
                    act.activation(sg[:, n], bank(n), ACT.Silu).then_inc(sg_ready, 1)
                for n in range(2):
                    act.wait_ge(h_ready, 2 * c + n + 1)
                    if c >= 2:
                        act.wait_ge(down_done, TILES * (c - 1))
                    act.copy(hh[0][:, c % 2, n * HALF:(n + 1) * HALF], h32[:, n]).then_inc(h_hi, 1)

        @block.vector
        def _(dve):
            count = {"stat": 0, "route": 0}

            def layernorm_stats(n, g):
                dve.bn_stats(stats[n][:, g, :], xs[:, g, :]).then_inc(stat_ready, 1)
                count["stat"] += 1
                dve.wait_ge(stat_ready, count["stat"])
                dve.bn_aggr(meanvar[n][:, g, :], stats[n][:, g, :]).then_inc(ln_stats[n], 1)

            def normalize(n, g, dst, ready):
                dve.wait_ge(rstd_ready[n], g + 1)
                dve.wait_ge(ln_stats[n], g + 1)
                dve.tensor_scalar(dst, xs[:, g, :], meanvar[n][:, g, 0:1], rstd[n][:, g:g + 1],
                                  ALU.subtract, ALU.mult).then_inc(ready, 1)

            def context_lo(g):
                dve.wait_ge(cx_hi, g + 1)
                if g >= 2:
                    dve.wait_ge(v_done, (GK // P) * (g - 1))
                dve.tensor_tensor(cx[1][:, g % 2], ctx_raw[g % 2][:, :, :], cx[0][:, g % 2].bitcast(F32),
                                  ALU.subtract).then_inc(cx_lo, 1)

            def chunk_lo(c):
                dve.wait_ge(wf_hi, c + 1)
                if c >= 2:
                    dve.wait_ge(down_done, TILES * (c - 1))
                dve.tensor_tensor(wf[1][:, c % 2, :], wf_raw[c % 2], wf[0][:, c % 2, :].bitcast(F32),
                                  ALU.subtract).then_inc(wf_lo, 1)

            def ln1_part(n):
                dve.wait_ge(ln1_hi, n + 1)
                cols = slice(n * 2 * P, (n + 1) * 2 * P)
                dve.tensor_tensor(lnt[1][:, :, cols].rearrange("p c (t m) -> p t c m", t=2),
                                  bank(4 + n).rearrange("p (t c m) -> p t c m", t=2, c=KC),
                                  lnt[0][:, :, cols].bitcast(F32).rearrange("p c (t m) -> p t c m", t=2),
                                  ALU.subtract).then_inc(ln1_lo, 1)

            dve.memset(minus_half[:, :], -0.5).then_inc(const_ready, 1)
            dve.memset(ones[:, :], 1.0).then_inc(const_ready, 1)
            for g in range(TILES):
                dve.wait_ge(d_x[g // (TILES // 2)], 16)
                layernorm_stats(0, g)
            for n in range(3):
                dve.wait_ge(wx_hi, n + 1)
                dve.tensor_tensor(wx[1][:, n], wx_raw[:, n], wx[0][:, n].bitcast(F32), ALU.subtract
                                  ).then_inc(wx_lo, 1)
                if n == 0:
                    for g in range(2):
                        normalize(0, g, xn1[:, g, :], xn1_ready)
            for g in range(2, TILES):
                dve.wait_ge(ln1_turned, g - 1)
                normalize(0, g, xn1[:, g % 2, :], xn1_ready)
                if g % 2 == 1:
                    ln1_part(g // 2 - 1)
            ln1_part(TILES // 2 - 1)
            context_lo(0)
            dve.wait_ge(d_const, 16 * 6)
            dve.tensor_scalar(g_shift[:, :], g_sb[:, :], -1.0, None, ALU.mult).then_inc(const_ready, 1)
            dve.tensor_scalar(bias_neg[:, :], bias_sb[:, :], -1.0, None, ALU.mult).then_inc(const_ready, 1)
            dve.wait_ge(const_ready, 4)
            dve.tensor_tensor(g_shift[:, :], g_shift[:, :], g_sb[:, :], ALU.min).then_inc(const_ready, 1)
            dve.wait_ge(const_ready, 5)
            dve.tensor_scalar(g_shift[:, :], g_shift[:, :], LIFT, None, ALU.add).then_inc(const_ready, 1)
            for half in range(2):
                for m in range(XP):
                    src = bank(2 * half + m).rearrange("p (b q) -> p b q", q=SEQ)
                    for j in range(2):
                        rows = slice(j * XD, (j + 1) * XD)
                        view = (rows, m, slice(half * 8, half * 8 + 8), slice(j * SEQ, (j + 1) * SEQ))
                        dve.wait_ge(q_hi, 4 * half + 2 * m + j + 1)
                        dve.scalar_tensor_tensor(out=qbd[1][view], in0=src[rows], scalar=XSCALE,
                                                 in1=qbd[0][view].bitcast(F32), op0=ALU.mult, op1=ALU.subtract
                                                 ).then_inc(q_lo, 1)
            dve.wait_ge(ws_hi, 1)
            dve.tensor_tensor(ws[1][:, :, :], ws_raw[:, :, :], ws[0][:, :, :].bitcast(F32), ALU.subtract
                              ).then_inc(ws_lo, 1)
            dve.wait_ge(zeroed, 9)
            dve.tensor_copy(gate_hl[0][:, :, 0:NE], gate_raw[:, :, :]).then_inc(const_ready, 1)
            dve.wait_ge(const_ready, 7)
            dve.tensor_tensor(gate_hl[1][:, :, 0:NE], gate_raw[:, :, :], gate_hl[0][:, :, 0:NE].bitcast(F32),
                              ALU.subtract).then_inc(const_ready, 1)

            def add_attention(g, psum, heads, hd, rs, scaled, rs_ready, scaled_ready, x_done):
                dve.reciprocal(rs[:, g, :], psum[:, :, hd]).then_inc(rs_ready, 1)
                dve.wait_ge(rs_ready, g + 1)
                if g >= 1:
                    dve.wait_ge(x_done, g)
                dve.tensor_tensor(scaled[:, :].rearrange("p (h d) -> p h d", h=heads), psum[:, :, 0:hd],
                                  rs[:, g, :].unsqueeze(2).to_broadcast([P, heads, hd]), ALU.mult
                                  ).then_inc(scaled_ready, 1)
                dve.wait_ge(scaled_ready, g + 1)
                dve.tensor_tensor(xs[:, g, :], xs[:, g, :], scaled[:, :], ALU.add).then_inc(x_done, 1)
                dve.wait_ge(x_done, g + 1)

            for i in range(SLOTS):
                g = tile_of(i, 1)
                if g is not None:
                    for b in range(GB):
                        dve.wait_ge(s_done, GB * g + b + 1)
                        dve.tensor_reduce(negmax[:, g, b, :], bank(4 + b).rearrange("p (m k) -> p m k", m=XP),
                                          AX.X, ALU.max, negate=True).then_inc(negmax_ready, 1)
                g = tile_of(i, 2)
                if g is not None:
                    if g >= 1:
                        dve.wait_ge(ln2_turned, g)
                    normalize(1, g, xn2[:, :], xn2_ready)
                g = tile_of(i, 5)
                if g is not None:
                    if g >= 1:
                        dve.wait_ge(ln3_turned, g)
                    normalize(2, g, xn3[:, :], xn3_ready)
                g = tile_of(i, 3)
                if g is not None:
                    dve.wait_ge(rnorm_ready, g + 1)
                    dve.wait_ge(raw_ready, g + 1)
                    if g >= 1:
                        dve.wait_ge(stack_ready, 2 * g)
                        dve.wait_ge(q_turned, g)
                        dve.wait_ge(k_turned, g)
                    dve.tensor_tensor(unit[:, :, :, :].rearrange("p a h d -> p (a h) d"),
                                      raw[:, :].rearrange("p (h d) -> p h d", d=SD),
                                      rnorm[:, g % 2, :].unsqueeze(2).to_broadcast([P, 2 * SH, SD]), ALU.mult
                                      ).then_inc(unit_ready, 1)
                    dve.wait_ge(unit_ready, g + 1)
                    for a in range(2):
                        src = unit[:, a].unsqueeze(2).to_broadcast([P, SH, 2, SD])
                        v = stack[a][:, :, :, :].rearrange("p h (u w) d -> p h u w d", u=2)
                        hi = v[:, :, :, 0, :] if a == 0 else v[:, :, 0, :, :]
                        dve.tensor_copy(hi, src).then_inc(stack_hi, 1)
                    for a in range(2):
                        src = unit[:, a].unsqueeze(2).to_broadcast([P, SH, 2, SD])
                        v = stack[a][:, :, :, :].rearrange("p h (u w) d -> p h u w d", u=2)
                        hi = v[:, :, :, 0, :] if a == 0 else v[:, :, 0, :, :]
                        lo = v[:, :, :, 1, :] if a == 0 else v[:, :, 1, :, :]
                        dve.wait_ge(stack_hi, 2 * g + a + 1)
                        dve.tensor_tensor(lo, src, hi, ALU.subtract).then_inc(stack_ready, 1)
                g = tile_of(i, 1)
                if g is not None:
                    for b in range(GB):
                        dve.wait_ge(exp_done, GB * g + b + 1)
                        if g >= 1:
                            dve.wait_ge(p_turned, GB * g)
                        dve.tensor_copy(ph[0][:, b], p32[:, b]).then_inc(p_hi, 1)
                g = tile_of(i, 4)
                if g is not None:
                    for b in range(GB):
                        dve.wait_ge(sexp_done, GB * g + b + 1)
                        if g >= 1:
                            dve.wait_ge(spv_done, g)
                        dve.tensor_copy(sh[0][:, b], s32[:, b]).then_inc(s_hi, 1)
                g = tile_of(i, 2)
                if g is not None:
                    dve.wait_ge(ln2_hi, g + 1)
                    dve.tensor_tensor(ln2t[1][:, :, :], bank(2)[:, 0:D].rearrange("p (c m) -> p c m", c=KC),
                                      ln2t[0][:, :, :].bitcast(F32), ALU.subtract).then_inc(ln2_lo, 1)
                g = tile_of(i, 5)
                if g is not None:
                    cols = slice(g * P, (g + 1) * P)
                    dve.wait_ge(ln3_hi, g + 1)
                    dve.tensor_tensor(lnt[1][:, :, cols], bank(3)[:, 0:D].rearrange("p (c m) -> p c m", c=KC),
                                      lnt[0][:, :, cols].bitcast(F32), ALU.subtract).then_inc(ln3_lo, 1)
                g = tile_of(i, 0)
                if g is not None:
                    for m in range(XP):
                        dve.wait_ge(k_hi, XP * g + m + 1)
                        dve.tensor_tensor(kt[1][:, m, :], bank(m), kt[0][:, m, :].bitcast(F32), ALU.subtract
                                          ).then_inc(k_lo, 1)
                if i + 1 < TILES:
                    context_lo(i + 1)
                if g is not None:
                    for n in range(2):
                        dve.wait_ge(v_hi, 2 * g + n + 1)
                        view = (slice(None), g % 2, slice(2 * n, 2 * n + 2), slice(None), slice(0, XD))
                        dve.tensor_tensor(vx[1][view], bank(3 - n).rearrange("p (t h d) -> p t h d", t=2, h=XH),
                                          vx[0][view], ALU.subtract).then_inc(v_lo, 1)
                g = tile_of(i, 2)
                if g is not None:
                    dve.wait_ge(sq_ready, g + 1)
                    dve.tensor_reduce(ss[:, :], sq[:, :].rearrange("p (h d) -> p h d", d=SD), AX.X, ALU.add
                                      ).then_inc(ss_sum, 1)
                    dve.wait_ge(ss_sum, g + 1)
                    if g >= 1:
                        dve.wait_ge(rnorm_ready, g)
                    dve.tensor_scalar(ssm[:, :], ss[:, :], EPS_NORM ** 2, None, ALU.max).then_inc(ss_ready, 1)
                    for b in range(GB):
                        for j in range(2):
                            src = bank(1)[b * SEQ:(b + 1) * SEQ, 0:D].rearrange("p (a j d) -> p a j d", j=2, d=SD)
                            view = (slice(j * SEQ, (j + 1) * SEQ), g % 3, b, slice(None), j, slice(0, SD))
                            dve.wait_ge(sv_hi, 4 * (g + 1))
                            dve.tensor_tensor(vbd[1][view], src[:, :, j], vbd[0][view], ALU.subtract
                                              ).then_inc(sv_lo, 1)
                g = tile_of(i, 1)
                if g is not None:
                    dve.wait_ge(pv_done, g + 1)
                    add_attention(g, bank(4)[:, 0:XH * (XD + 1)].rearrange("p (h d) -> p h d", h=XH), XH, XD,
                                  rsum, att, rsum_ready, att_ready, x_cross)
                    layernorm_stats(1, g)
                g = tile_of(i, 4)
                if g is not None:
                    dve.wait_ge(spv_done, g + 1)
                    add_attention(g, bank(6)[:, 0:SH * (SD + 1)].rearrange("p (h d) -> p h d", h=SH), SH, SD,
                                  rsum2, att2, rsum2_ready, att2_ready, x_self)
                    layernorm_stats(2, g)
                g = tile_of(i, 3)
                if g is not None:
                    dve.wait_ge(q_turned, g + 1)
                    dve.tensor_copy(qt[:, :, :].rearrange("p a q -> p (a q)"), bank(7).bitcast(F16)
                                    ).then_inc(qt_ready, 1)
                if i in (SLOTS - 3, SLOTS - 2):
                    chunk_lo(i - (SLOTS - 3))

            def step(ins):
                ins.then_inc(route, 1)
                count["route"] += 1
                dve.wait_ge(route, count["route"])

            def over_experts(a):
                return a[:, :].unsqueeze(2).to_broadcast([P, TILES, NE])

            def over_tiles(a):
                return a[:, :].unsqueeze(1).to_broadcast([P, TILES, NE])

            def pick_first(src, best, hot):
                step(dve.tensor_reduce(best[:, :], src[:, :, :], AX.X, ALU.max))
                step(dve.tensor_tensor(r1[:, :, :], src[:, :, :], over_experts(best), ALU.is_equal))
                step(dve.tensor_tensor(r1[:, :, :], r1[:, :, :], rank_sb[:, :, :], ALU.mult))
                step(dve.tensor_reduce(pick[:, :], r1[:, :, :], AX.X, ALU.max))
                step(dve.tensor_tensor(hot[:, :, :], r1[:, :, :], over_experts(pick), ALU.is_equal))

            def gate_times_up(c):
                for n in range(2):
                    dve.wait_ge(sg_ready, 2 * c + n + 1)
                    dve.wait_ge(up_done, 2 * c + n + 1)
                    if c >= 1:
                        dve.wait_ge(h_hi, 2 * (c - 1) + n + 1)
                        dve.wait_ge(h_lo, 2 * (c - 1) + n + 1)
                    dve.tensor_tensor(h32[:, n], sg[:, n], bank(2 + n), ALU.mult).then_inc(h_ready, 1)
                for n in range(2):
                    dve.wait_ge(h_hi, 2 * c + n + 1)
                    dve.tensor_tensor(hh[1][:, c % 2, n * HALF:(n + 1) * HALF], h32[:, n],
                                      hh[0][:, c % 2, n * HALF:(n + 1) * HALF].bitcast(F32), ALU.subtract
                                      ).then_inc(h_lo, 1)

            def add_chunk(c):
                for t in range(TILES):
                    dve.wait_ge(down_done, TILES * c + 2 * (t // 2) + 2)
                    if c >= 1:
                        dve.wait_ge(x_ffn, TILES * (c - 1) + t + 1)
                    y = bank(4 + t // 2)[:, (t % 2) * D:(t % 2 + 1) * D]
                    if c < SHARED:
                        ins = dve.tensor_tensor(xs[:, t, :], y, xs[:, t, :], ALU.add)
                    else:
                        ins = dve.scalar_tensor_tensor(out=xs[:, t, :], in0=y,
                                                       scalar=coef[:, t, c - SHARED:c - SHARED + 1],
                                                       in1=xs[:, t, :], op0=ALU.mult, op1=ALU.add)
                    ins.then_inc(x_ffn, 1)

            dve.wait_ge(s_lo, GB * TILES)
            gate_times_up(0)
            dve.wait_ge(e_turned, TILES)
            step(dve.tensor_scalar(r1[:, :, :], bank(6)[:, 0:TILES * NE].rearrange("p (t e) -> p t e", t=TILES),
                                   1.0, None, ALU.add))
            step(dve.reciprocal(S[:, :, :], r1[:, :, :]))
            pick_first(S, top[0], onehot[0])
            step(dve.scalar_tensor_tensor(out=rest[:, :, :], in0=onehot[0][:, :, :], scalar=-2.0, in1=S[:, :, :],
                                          op0=ALU.mult, op1=ALU.add))
            pick_first(rest, top[1], onehot[1])
            step(dve.tensor_tensor(den[:, :], top[0][:, :], top[1][:, :], ALU.add))
            step(dve.tensor_scalar(den[:, :], den[:, :], 1e-8, None, ALU.add))
            step(dve.reciprocal(rden[:, :], den[:, :]))
            step(dve.tensor_tensor(tally[:, :, 1, :], onehot[0][:, :, :], onehot[1][:, :, :], ALU.add))
            step(dve.tensor_tensor(r1[:, :, :], S[:, :, :], tally[:, :, 1, :], ALU.mult))
            dve.tensor_tensor(tally[:, :, 0, :], r1[:, :, :], over_experts(rden), ALU.mult).then_inc(tally_ready, 1)
            gate_times_up(1)
            dve.wait_ge(tally_done, 1)
            step(dve.tensor_reduce(total[:, :], bank(7)[:, 0:TILES * 2 * NE].rearrange("p (t e) -> p e t", t=TILES),
                                   AX.X, ALU.add))
            step(dve.tensor_scalar(cnt[:, :], total[:, NE:], 1.0, None, ALU.max))
            step(dve.reciprocal(rcnt[:, :], cnt[:, :]))
            step(dve.tensor_tensor(wmean[:, :], total[:, 0:NE], rcnt[:, :], ALU.mult))
            step(dve.tensor_tensor(coef[:, :, :], tally[:, :, 1, :], over_tiles(wmean), ALU.mult))
            for c in range(CHUNKS):
                if 2 <= c + 1 < CHUNKS:
                    gate_times_up(c + 1)
                add_chunk(c)
                if c + 2 < CHUNKS:
                    chunk_lo(c + 2)

        @block.tensor
        def _(pe):
            def product(dst, lhs, rhs, k):
                n = 0
                for c in range(k):
                    for a, b in PARTS:
                        mm = pe.matmul(dst, lhs(a, c), rhs(b, c), start=(n == 0), stop=(n == 3 * k - 1))
                        n += 1
                return mm

            pe.wait_ge(d_const, 16 * 6)
            for t in range(TILES):
                pe.wait_ge(xn1_ready, t + 1)
                for c in range(KC):
                    o = ((t % 2) * KC + c) * P
                    mm = pe.transpose(bank(4 + t // 2)[:, o:o + P], xn1[:, t % 2, c * P:(c + 1) * P], id32[:, :])
                mm.then_inc(ln1_turned, 1)
            pe.wait_ge(wx_lo, 1)
            for half in range(2):
                pe.wait_ge(ln1_lo, 2 * (half + 1))
                for m in range(XP):
                    product(bank(2 * half + m),
                            lambda a, c: wx[a][:, 0, c, m * P:(m + 1) * P],
                            lambda b, c: lnt[b][:, c, half * HALF:(half + 1) * HALF], KC).then_inc(q_done, 1)

            for i in range(SLOTS):
                g = tile_of(i, 1)
                if g is not None:
                    pe.wait_ge(k_lo, XP * (g + 1))
                    for b in range(GB):
                        if g >= 1:
                            pe.wait_ge(att_ready, g) if b == 0 else None
                        if b == 1 and tile_of(i - 1, 3) is not None:
                            pe.wait_ge(kbd_ready, 2 * (tile_of(i - 1, 3) + 1))
                        for m in range(XP):
                            mm = product(bank(4 + b)[:, m * CTX:(m + 1) * CTX],
                                         lambda a, c: qbd[a][:, m, GB * g + b, :],
                                         lambda r, c: kt[r][:, m, b * CTX:(b + 1) * CTX], 1)
                        mm.then_inc(s_done, 1)
                g = tile_of(i, 4)
                if g is not None:
                    pe.wait_ge(kbd_ready, 2 * (g + 1))
                    pe.wait_ge(qt_ready, g + 1)
                    if g >= 1:
                        pe.wait_ge(att2_ready, g)
                    for b in range(GB):
                        for a in range(SP_):
                            mm = pe.matmul(bank(6 + b)[:, a * SEQ:(a + 1) * SEQ], kbd[:, a, b, :, :],
                                           qt[:, a, b * SEQ:(b + 1) * SEQ], start=True, stop=True)
                        mm.then_inc(ss_done, 1)
                g = tile_of(i, 0)
                if g is not None:
                    pe.wait_ge(wx_lo, 2)
                    pe.wait_ge(cx_lo, g + 1)
                    if i == 0:
                        pe.wait_ge(q_lo, 4)
                    last = tile_of(i - 1, 2)
                    if last is not None:
                        pe.wait_ge(sq_ready, last + 1)
                        pe.wait_ge(sv_lo, 4 * (last + 1))
                    for m in range(XP):
                        product(bank(m), lambda a, c: wx[a][:, 1, c, m * P:(m + 1) * P],
                                lambda b, c: cx[b][:, g % 2, c, :], KC).then_inc(k_done, 1)
                if i == 0:
                    pe.wait_ge(q_lo, 8)
                if g is not None and g >= 1:
                    pe.wait_ge(v_lo, 2 * g)
                elif g is None:
                    pe.wait_ge(v_lo, 2 * TILES)
                g = tile_of(i, 2)
                if g is not None:
                    pe.wait_ge(xn2_ready, g + 1)
                    for c in range(KC):
                        mm = pe.transpose(bank(2)[:, c * P:(c + 1) * P], xn2[:, c * P:(c + 1) * P], id32[:, :])
                    mm.then_inc(ln2_turned, 1)
                g = tile_of(i, 5)
                if g is not None:
                    pe.wait_ge(xn3_ready, g + 1)
                    if g >= 1:
                        pe.wait_ge(ln3_lo, g)
                    for c in range(KC):
                        mm = pe.transpose(bank(3)[:, c * P:(c + 1) * P], xn3[:, c * P:(c + 1) * P],
                                          id32[:, :])
                    mm.then_inc(ln3_turned, 1)
                g = tile_of(i, 1)
                if g is not None:
                    for b in range(GB):
                        pe.wait_ge(p_lo, GB * g + b + 1)
                        v = bank(4 + b).bitcast(F16)
                        for s in range(2):
                            for c in range(KC):
                                for m in range(XP):
                                    o = ((s * KC + c) * XP + m) * P
                                    mm = pe.transpose(v[:, o:o + P], ph[s][:, b, m, c * P:(c + 1) * P], id16[:, :])
                        mm.then_inc(p_turned, 1)
                g = tile_of(i, 0)
                if g is not None:
                    pe.wait_ge(wx_lo, 3)
                    for t in range(GK // P):
                        if t == 0 and tile_of(i, 5) is not None:
                            pe.wait_ge(ln3_lo, tile_of(i, 5) + 1)
                        if t == 2 and tile_of(i, 2) is not None:
                            pe.wait_ge(ln2_lo, tile_of(i, 2) + 1)
                        product(bank(3 - t // 2)[:, (t % 2) * D:(t % 2 + 1) * D],
                                lambda a, c: cx[a][:, g % 2, c, t * P:(t + 1) * P],
                                lambda b, c: wx[b][:, 2, c, :], KC).then_inc(v_done, 1)
                g = tile_of(i, 2)
                if g is not None:
                    pe.wait_ge(ws_lo, 1)
                    pe.wait_ge(ln2_lo, g + 1)
                    pe.wait_ge(k_lo, XP * (min(i, TILES - 1) + 1))
                    if g >= 1:
                        pe.wait_ge(sv_lo, 4 * g)
                        pe.wait_ge(sq_ready, g)
                    for n, (lo, hi) in enumerate(((0, 2 * D), (2 * D, 3 * D))):
                        product(bank(n)[:, 0:hi - lo], lambda a, c: ln2t[a][:, c, :],
                                lambda b, c: ws[b][:, c, lo:hi], KC).then_inc(qkv_done, 1)
                g = tile_of(i, 1)
                if g is not None:
                    pe.wait_ge(pt_ready, GB * (g + 1))
                    pe.wait_ge(v_lo, 2 * (g + 1))
                    for b in range(GB):
                        for h in range(XH):
                            mm = product(bank(4)[b * SEQ:(b + 1) * SEQ, h * (XD + 1):(h + 1) * (XD + 1)],
                                         lambda a, c: pt[:, b, a, c, h, :],
                                         lambda r, c: vx[r][:, g % 2, b * KC + c, h, :], KC)
                    mm.then_inc(pv_done, 1)
                g = tile_of(i, 4)
                if g is not None:
                    pe.wait_ge(s_lo, GB * (g + 1))
                    pe.wait_ge(sv_lo, 4 * (g + 1))
                    for b in range(GB):
                        for a in range(SP_):
                            w = 2 * (SD + 1)
                            mm = product(bank(6)[b * SEQ:(b + 1) * SEQ, a * w:(a + 1) * w],
                                         lambda s, c: sh[s][:, b, a, :],
                                         lambda r, c: vbd[r][:, g % 3, b, a, :, :], 1)
                    mm.then_inc(spv_done, 1)
                g = tile_of(i, 3)
                if g is not None:
                    if tile_of(i, 4) is not None:
                        pe.wait_ge(sexp_done, GB * (tile_of(i, 4) + 1))
                    if i - 1 >= TILES:
                        pe.wait_ge(pt_ready, GB * TILES)
                    for n, (st, b, turned) in enumerate(((stack[0], 7, q_turned), (stack[1], 5, k_turned))):
                        pe.wait_ge(stack_ready, 2 * g + n + 1)
                        if g >= 1:
                            pe.wait_ge(qt_ready, g) if n == 0 else pe.wait_ge(kbd_ready, 2 * g)
                        v = bank(b).bitcast(F16)
                        flat = st[:, :, :, :].rearrange("p h u d -> p (h u d)")
                        for a in range(SP_):
                            mm = pe.transpose(v[:, a * P:(a + 1) * P], flat[:, a * P:(a + 1) * P], id16[:, :])
                        mm.then_inc(turned, 1)

            pe.wait_ge(const_ready, 8)
            for n in range(2):
                pe.wait_ge(ln3_lo, (n + 1) * TILES // 2)
                product(bank(4 + n), lambda a, c: gate_hl[a][:, c, :],
                        lambda b, c: lnt[b][:, c, n * HALF:(n + 1) * HALF], KC).then_inc(logits_done, 1)

            def gate_and_up(c):
                pe.wait_ge(wf_lo, c + 1)
                for n in range(2):
                    for u, done in enumerate((gate_done, up_done)):
                        if c >= 1:
                            pe.wait_ge(sg_ready, 2 * (c - 1) + n + 1) if u == 0 else \
                                pe.wait_ge(h_ready, 2 * (c - 1) + n + 1)
                        product(bank(2 * u + n),
                                lambda a, k: wf[a][:, c % 2, (u * KC + k) * CH:(u * KC + k + 1) * CH],
                                lambda b, k: lnt[b][:, k, n * HALF:(n + 1) * HALF], KC).then_inc(done, 1)

            def down(c):
                pe.wait_ge(h_lo, 2 * (c + 1))
                for t in range(TILES):
                    if c >= 1:
                        pe.wait_ge(x_ffn, TILES * (c - 1) + 2 * (t // 2) + 2)
                    product(bank(4 + t // 2)[:, (t % 2) * D:(t % 2 + 1) * D],
                            lambda a, k: hh[a][:, c % 2, t * P:(t + 1) * P],
                            lambda b, k: wf[b][:, c % 2, 2 * KC * CH:], 1).then_inc(down_done, 1)

            gate_and_up(0)
            for t in range(TILES):
                pe.wait_ge(et_ready, t // (TILES // 2) + 1)
                pe.transpose(bank(6)[:, t * NE:(t + 1) * NE], et[:, t * P:(t + 1) * P], id32[0:NE, 0:NE]
                             ).then_inc(e_turned, 1)
            gate_and_up(1)
            pe.wait_ge(tally_ready, 1)
            pe.matmul(bank(7)[:, 0:TILES * 2 * NE], ones[:, :], tally[:, :, :, :], start=True, stop=True
                      ).then_inc(tally_done, 1)
            pe.wait_ge(et_ready, 2)
            pe.wait_ge(route, 1)
            for c in range(CHUNKS):
                if 2 <= c + 1 < CHUNKS:
                    gate_and_up(c + 1)
                if c == 0:
                    pe.wait_ge(route, ROUTE_TOTALS)
                down(c)


ROUTE_TOTALS = 2 + 5 + 1 + 5 + 5 + 1


def kernel(x, ctx_1024, L0_xattn_Wq, L0_xattn_Wk, L0_xattn_Wv, L0_attn_Wq, L0_attn_Wk, L0_attn_Wv,
           L0_attn_g_scale, L0_ffn_gate_w, L0_ffn_lb_bias, L0_ffn_expert_gate_w, L0_ffn_expert_up_w,
           L0_ffn_expert_down_w, L0_ffn_shared_gate_w, L0_ffn_shared_up_w, L0_ffn_shared_down_w):
    import numpy as np
    import concourse.bacc as bacc
    from concourse.bass_utils import run_bass_kernel_spmd

    def chunks(w):
        w = np.asarray(w)
        return w.T.reshape(w.shape[1] // P, P, w.shape[0]).transpose(1, 0, 2)

    def chunk_weights(gate, up, down):
        return np.concatenate([chunks(gate).reshape(P, -1), chunks(up).reshape(P, -1), np.asarray(down).T], axis=1)

    ctx_t = np.asarray(ctx_1024).reshape(TILES, GB, CTX, KC, P).transpose(0, 4, 3, 1, 2).reshape(TILES, P, KC, GK)
    sg, su, sd = (np.asarray(a) for a in (L0_ffn_shared_gate_w, L0_ffn_shared_up_w, L0_ffn_shared_down_w))
    eg, eu, ed = (np.asarray(a) for a in (L0_ffn_expert_gate_w, L0_ffn_expert_up_w, L0_ffn_expert_down_w))
    w_ffn = [chunk_weights(sg[n * CH:(n + 1) * CH], su[n * CH:(n + 1) * CH], sd[:, n * CH:(n + 1) * CH])
             for n in range(SHARED)]
    w_ffn += [chunk_weights(eg[n], eu[n], ed[n]) for n in range(NE)]
    arrays = {
        "x_tokens": np.asarray(x).reshape(TOK, D),
        "ctx_t": ctx_t,
        "w_cross": np.stack([chunks(w) for w in (L0_xattn_Wq, L0_xattn_Wk, L0_xattn_Wv)], axis=1),
        "w_self": np.concatenate([chunks(w) for w in (L0_attn_Wq, L0_attn_Wk, L0_attn_Wv)], axis=2),
        "g_scale": np.broadcast_to(np.asarray(L0_attn_g_scale).reshape(1, 1), (P, 1)),
        "gate_w": chunks(L0_ffn_gate_w),
        "lb_bias": np.asarray(L0_ffn_lb_bias).reshape(NE, 1),
        "w_ffn": np.stack(w_ffn),
        "ident32": np.eye(P, dtype=np.float32),
        "ident16": np.eye(P, dtype=np.float16),
        "rank": np.broadcast_to(np.arange(NE, 0, -1, dtype=np.float32), (P, TILES, NE)),
    }
    arrays = {k: np.ascontiguousarray(v) for k, v in arrays.items()}
    nc = bacc.Bacc("TRN2", target_bir_lowering=False, num_devices=1)
    args = [nc.dram_tensor(k, v.shape, mybir.dt.from_np(v.dtype), kind="ExternalInput").ap()
            for k, v in arrays.items()]
    out = nc.dram_tensor("out", (TOK, D), F32, kind="ExternalOutput").ap()
    build(nc, *args, out)
    r = run_bass_kernel_spmd(nc, [arrays], core_ids=[0])
    return r.results[0]["out"].reshape(BATCH, SEQ, D)
```

```python
from contextlib import ExitStack

import concourse.bass as bass
from concourse import mybir

ALU = mybir.AluOpType
ACT = mybir.ActivationFunctionType
AX = mybir.AxisListType
F32 = mybir.dt.float32
F32R = mybir.dt.float32r
F16 = mybir.dt.float16

P = 128
D = 256
KC = D // P
BATCH = 16
SEQ = 64
CTX = 256
TOK = BATCH * SEQ
TILES = TOK // P
GB = P // SEQ
GK = GB * CTX
XH = 4
XD = D // XH
XP = XH // 2
SH = 16
SD = D // SH
SP_ = SH // 2
NE = 8
CH = 128
SHARED = 2
CHUNKS = SHARED + NE
WC = 2 * KC * CH + D
WBUF = 4
HALF = TOK // 2
EPS_LN = 1e-5
EPS_NORM = 1e-12
XSCALE = float(XD) ** -0.5
LOG_LIFT = 2.0 ** 20
HALF_LOG = 6.931471805599453
LIFT = 8.317766166719343

PARTS = ((0, 0), (0, 1), (1, 0))


def build(nc, x, ctx_t, w_cross, w_self, g_scale, gate_w, lb_bias, w_ffn, ident32, ident16, rank, out):
    with ExitStack() as ctx:
        def sb(name, shape, dt=F32):
            return ctx.enter_context(nc.sbuf_tensor(name, shape, dt))

        def sem(name):
            return ctx.enter_context(nc.semaphore(name))

        id32 = sb("id32", [P, P])
        id16 = sb("id16", [P, P], F16)
        rank_sb = sb("rank_sb", [P, TILES, NE])
        ones = sb("ones", [P, P])
        minus_half = sb("minus_half", [P, 2 * SH])
        g_sb = sb("g_sb", [P, 1])
        g_shift = sb("g_shift", [P, 1])
        half_log = sb("half_log", [P, 1])
        bias_sb = sb("bias_sb", [NE, 1])
        bias_neg = sb("bias_neg", [NE, 1])
        gate_raw = sb("gate_raw", [P, KC, NE])
        gate_hl = [sb(f"gate_{n}", [P, KC, P], F32R) for n in ("hi", "lo")]
        xs = sb("xs", [P, TILES, D])
        wx_raw = sb("wx_raw", [P, 3, KC, D])
        wx = [sb(f"wx_{n}", [P, 3, KC, D], F32R) for n in ("hi", "lo")]
        ws_raw = sb("ws_raw", [P, KC, 3 * D])
        ws = [sb(f"ws_{n}", [P, KC, 3 * D], F32R) for n in ("hi", "lo")]
        stats = [sb(f"stats{n}", [P, TILES, 6]) for n in range(3)]
        meanvar = [sb(f"meanvar{n}", [P, TILES, 2]) for n in range(3)]
        veps = [sb(f"veps{n}", [P, TILES]) for n in range(3)]
        rstd = [sb(f"rstd{n}", [P, TILES]) for n in range(3)]
        xn1 = sb("xn1", [P, 2, D])
        xn2 = sb("xn2", [P, D])
        xn3 = sb("xn3", [P, D])
        lnt = [sb(f"lnt_{n}", [P, KC, TOK], F32R) for n in ("hi", "lo")]
        ln2t = [sb(f"ln2t_{n}", [P, KC, P], F32R) for n in ("hi", "lo")]
        ctx_raw = [sb(f"ctx_raw{n}", [P, KC, GK]) for n in range(2)]
        cx = [sb(f"cx_{n}", [P, 2, KC, GK], F32R) for n in ("hi", "lo")]
        qbd = [sb(f"qbd_{n}", [P, XP, BATCH, P], F32R) for n in ("hi", "lo")]
        kt = [sb(f"kt_{n}", [P, XP, GK], F32R) for n in ("hi", "lo")]
        vx = [sb(f"vx_{n}", [P, 2, GK // P, XH, XD + 1], F16) for n in ("hi", "lo")]
        negmax = sb("negmax", [P, TILES, GB, XP])
        p32 = sb("p32", [P, GB, XP, CTX])
        ph = [sb(f"p_{n}", [P, GB, XP, CTX], F16) for n in ("hi", "lo")]
        pt = sb("pt", [P, GB, 2, KC, XH, SEQ], F16)
        rsum = sb("rsum", [P, TILES, XH])
        att = sb("att", [P, D])
        raw = sb("raw", [P, 2 * D])
        sq = sb("sq", [P, 2 * D])
        ss = sb("ss", [P, 2 * SH])
        ssm = sb("ssm", [P, 2 * SH])
        logs = sb("logs", [P, 2 * SH])
        guess = sb("guess", [P, 2 * SH])
        newton = sb("newton", [P, 2 * SH])
        rnorm = sb("rnorm", [P, 2, 2 * SH])
        unit = sb("unit", [P, 2, SH, SD])
        stack = [sb(f"stack_{n}", [P, SH, 4, SD], F16) for n in ("q", "k")]
        qt = sb("qt", [P, SP_, P], F16)
        kbd = sb("kbd", [P, SP_, GB, 2, SEQ], F16)
        vbd = [sb(f"vbd_{n}", [P, 3, GB, SP_, 2, SD + 1], F16) for n in ("hi", "lo")]
        s32 = sb("s32", [P, GB, SP_, SEQ])
        sh = [sb(f"s_{n}", [P, GB, SP_, SEQ], F16) for n in ("hi", "lo")]
        rsum2 = sb("rsum2", [P, TILES, SH])
        att2 = sb("att2", [P, D])
        et = sb("et", [NE, TOK])
        S = sb("S", [P, TILES, NE])
        r1 = sb("r1", [P, TILES, NE])
        onehot = [sb(f"onehot{n}", [P, TILES, NE]) for n in range(2)]
        rest = sb("rest", [P, TILES, NE])
        top = [sb(f"top{n}", [P, TILES]) for n in range(2)]
        pick = sb("pick", [P, TILES])
        den = sb("den", [P, TILES])
        rden = sb("rden", [P, TILES])
        tally = sb("tally", [P, TILES, 2, NE])
        total = sb("total", [P, 2 * NE])
        cnt = sb("cnt", [P, NE])
        rcnt = sb("rcnt", [P, NE])
        wmean = sb("wmean", [P, NE])
        coef = sb("coef", [P, TILES, NE])
        wf_raw = [wx_raw[:, :, :, :].rearrange("p a c n -> p (a c n)")[:, n * WC:(n + 1) * WC] for n in range(2)]
        wf_own = [sb(f"wf_{n}", [P, 2, WC], F32R) for n in ("hi", "lo")]
        wf = [[wf_own[n][:, 0, :], wf_own[n][:, 1, :]]
              + [cx[n][:, u].rearrange("p c k -> p (c k)")[:, 0:WC] for u in range(2)] for n in range(2)]
        sg = p32[:, :, :, :].rearrange("p b m k -> p b (m k)")
        h32 = s32[:, :, :, :].rearrange("p b a q -> p b (a q)")
        hh = [qbd[n][:, :, :, :].rearrange("p m b q -> p (m b q)")[:, 0:2 * TOK].rearrange("p (u t) -> p u t", u=2)
              for n in range(2)]

        ps = ctx.enter_context(nc.psum_tensor("ps", [P, 8, 512], F32))

        def bank(b):
            return ps[:, b, :]

        d_const = sem("d_const")
        d_x = [sem(f"d_x{n}") for n in range(2)]
        d_wx = [sem(f"d_wx{n}") for n in range(3)]
        d_ws = sem("d_ws")
        d_ctx = [sem(f"d_ctx{n}") for n in range(2)]
        d_wf = [sem(f"d_wf{n}") for n in range(2)]
        d_out = sem("d_out")
        zeroed = sem("zeroed")
        pool_veps = sem("pool_veps")
        rstd_ready = [sem(f"rstd{n}_ready") for n in range(3)]
        wx_hi, wx_lo = sem("wx_hi"), sem("wx_lo")
        ws_hi, ws_lo = sem("ws_hi"), sem("ws_lo")
        cx_hi, cx_lo = sem("cx_hi"), sem("cx_lo")
        wf_hi, wf_lo = sem("wf_hi"), sem("wf_lo")
        p_lo, s_lo, p_hi, s_hi = sem("p_lo"), sem("s_lo"), sem("p_hi"), sem("s_hi")
        newton_step, rnorm_ready = sem("newton_step"), sem("rnorm_ready")
        ln1_turned = sem("ln1_turned")
        q_done = sem("q_done")
        s_done, ss_done = sem("s_done"), sem("ss_done")
        k_done, v_done = sem("k_done"), sem("v_done")
        ln2_turned, ln3_turned = sem("ln2_turned"), sem("ln3_turned")
        p_turned, pv_done, spv_done = sem("p_turned"), sem("pv_done"), sem("spv_done")
        qkv_done = sem("qkv_done")
        q_turned, k_turned = sem("q_turned"), sem("k_turned")
        logits_done, e_turned, tally_done = sem("logits_done"), sem("e_turned"), sem("tally_done")
        gate_done, up_done, down_done = sem("gate_done"), sem("up_done"), sem("down_done")
        ln1_hi, q_hi = sem("ln1_hi"), sem("q_hi")
        exp_done, sexp_done = sem("exp_done"), sem("sexp_done")
        ln2_hi, ln3_hi = sem("ln2_hi"), sem("ln3_hi")
        k_hi, v_hi, pt_ready = sem("k_hi"), sem("v_hi"), sem("pt_ready")
        raw_ready, sq_ready, sv_hi = sem("raw_ready"), sem("sq_ready"), sem("sv_hi")
        log_ready, guess_ready = sem("log_ready"), sem("guess_ready")
        kbd_ready, et_ready = sem("kbd_ready"), sem("et_ready")
        sg_ready, h_hi = sem("sg_ready"), sem("h_hi")
        const_ready = sem("const_ready")
        stat_ready = sem("stat_ready")
        ln_stats = [sem(f"ln{n}_stats") for n in range(3)]
        xn1_ready, xn2_ready, xn3_ready = sem("xn1_ready"), sem("xn2_ready"), sem("xn3_ready")
        ln1_lo, q_lo = sem("ln1_lo"), sem("q_lo")
        negmax_ready = sem("negmax_ready")
        unit_ready, stack_hi, stack_ready = sem("unit_ready"), sem("stack_hi"), sem("stack_ready")
        ln2_lo, ln3_lo = sem("ln2_lo"), sem("ln3_lo")
        k_lo, v_lo, sv_lo = sem("k_lo"), sem("v_lo"), sem("sv_lo")
        ss_sum, ss_ready = sem("ss_sum"), sem("ss_ready")
        rsum_ready, att_ready, x_cross = sem("rsum_ready"), sem("att_ready"), sem("x_cross")
        rsum2_ready, att2_ready, x_self = sem("rsum2_ready"), sem("att2_ready"), sem("x_self")
        qt_ready = sem("qt_ready")
        route = sem("route")
        tally_ready, coef_ready = sem("tally_ready"), sem("coef_ready")
        h_ready, h_lo, x_ffn = sem("h_ready"), sem("h_lo"), sem("x_ffn")

        SLOTS = TILES + 5

        def tile_of(slot, lag):
            g = slot - lag
            return g if 0 <= g < TILES else None

        block = ctx.enter_context(nc.Block())

        @block.sync
        def _(sp):
            sp.dma_start(wx_raw[:, 1], w_cross[:, 1]).then_inc(d_wx[1], 16)
            sp.dma_start(ctx_raw[0][:, :, :], ctx_t[0]).then_inc(d_ctx[0], 16)
            for n in range(2):
                h = TILES // 2
                sp.dma_start(xs[:, n * h:(n + 1) * h, :],
                             x.rearrange("(t p) d -> p t d", p=P)[:, n * h:(n + 1) * h, :]).then_inc(d_x[n], 16)
            for n in (2, 0):
                sp.dma_start(wx_raw[:, n], w_cross[:, n]).then_inc(d_wx[n], 16)
            for dst, src in ((id32[:, :], ident32), (id16[:, :], ident16), (rank_sb[:, :, :], rank),
                             (g_sb[:, :], g_scale), (bias_sb[:, :], lb_bias), (gate_raw[:, :, :], gate_w)):
                sp.dma_start(dst, src).then_inc(d_const, 16)
            for g in range(1, TILES):
                if g == 2:
                    sp.dma_start(ws_raw[:, :, :], w_self).then_inc(d_ws, 16)
                if g >= 2:
                    sp.wait_ge(cx_lo, g - 1)
                sp.dma_start(ctx_raw[g % 2][:, :, :], ctx_t[g]).then_inc(d_ctx[g % 2], 16)
            for c in range(CHUNKS):
                if c == 0:
                    sp.wait_ge(wx_lo, 3)
                if c >= 2:
                    sp.wait_ge(wf_lo, c - 1)
                sp.dma_start(wf_raw[c % 2], w_ffn[c]).then_inc(d_wf[c % 2], 16)
            for n in range(TILES // 2):
                sp.wait_ge(x_ffn, (CHUNKS - 1) * TILES + 2 * n + 2)
                sp.dma_start(out.rearrange("(t p) d -> p t d", p=P)[:, 2 * n:2 * n + 2, :],
                             xs[:, 2 * n:2 * n + 2, :]).then_inc(d_out, 16)
            sp.wait_ge(d_out, 16 * (TILES // 2))

        @block.gpsimd
        def _(pool):
            def split_hi(dst, src):
                return pool.tensor_scalar(dst, src, 1.0, 0.0, ALU.mult, ALU.add)

            def inverse_std(n, g0, g1, stats_done):
                pool.wait_ge(ln_stats[n], stats_done)
                pool.tensor_scalar(veps[n][:, g0:g1], meanvar[n][:, g0:g1, 1], 1.0, EPS_LN, ALU.mult, ALU.add
                                   ).then_inc(pool_veps, 1)
                count["veps"] += 1
                pool.wait_ge(pool_veps, count["veps"])
                pool.tensor_tensor(rstd[n][:, g0:g1], veps[n][:, g0:g1], minus_half[:, 0:g1 - g0], ALU.pow
                                   ).then_inc(rstd_ready[n], g1 - g0)

            count = {"veps": 0}

            def context_hi(g):
                pool.wait_ge(d_ctx[g % 2], 16 * (g // 2 + 1))
                if g >= 2:
                    pool.wait_ge(v_done, (GK // P) * (g - 1))
                split_hi(cx[0][:, g % 2], ctx_raw[g % 2][:, :, :]).then_inc(cx_hi, 1)

            def context_lo(g):
                pool.wait_ge(cx_hi, g + 1)
                pool.tensor_tensor(cx[1][:, g % 2], ctx_raw[g % 2][:, :, :], cx[0][:, g % 2].bitcast(F32),
                                   ALU.subtract).then_inc(cx_lo, 1)

            def chunk_hi(c):
                pool.wait_ge(d_wf[c % 2], 16 * (c // 2 + 1))
                if c >= 2:
                    pool.wait_ge(v_done, (GK // P) * TILES)
                if c >= WBUF:
                    pool.wait_ge(down_done, TILES * (c - WBUF + 1))
                split_hi(wf[0][c % WBUF], wf_raw[c % 2]).then_inc(wf_hi, 1)

            pool.memset(qbd[1][:, :, :, :].bitcast(F32), 0.0).then_inc(zeroed, 1)
            context_hi(0)
            pool.wait_ge(const_ready, 2)
            inverse_std(0, 0, TILES // 2, TILES // 2)
            inverse_std(0, TILES // 2, TILES, TILES)
            pool.memset(vx[1][:, :, :, :, XD:], 0.0).then_inc(zeroed, 1)
            pool.memset(vx[0][:, :, :, :, XD:], 1.0).then_inc(zeroed, 1)
            context_hi(1)
            context_lo(1)
            for n in range(2):
                pool.memset(gate_hl[n][:, :, :].bitcast(F32), 0.0).then_inc(zeroed, 1)
            pool.memset(kbd[:, :, :, :, :].bitcast(F32), 0.0).then_inc(zeroed, 1)
            for n in range(2):
                pool.memset(vbd[n][:, :, :, :, :, :], 0.0).then_inc(zeroed, 1)
            pool.wait_ge(zeroed, 8)
            for j in range(2):
                rows = slice(j * SEQ, (j + 1) * SEQ)
                pool.memset(vbd[0][rows, :, :, :, j, SD:], 1.0).then_inc(zeroed, 1)
                pool.wait_ge(zeroed, 9 + j)
            pool.wait_ge(d_ws, 16)
            split_hi(ws[0][:, :, :], ws_raw[:, :, :]).then_inc(ws_hi, 1)

            for i in range(SLOTS):
                g = tile_of(i, 1)
                if g is not None:
                    for b in range(GB):
                        pool.wait_ge(p_hi, GB * g + b + 1)
                        if g >= 1:
                            pool.wait_ge(p_turned, GB * g)
                        pool.tensor_tensor(ph[1][:, b], p32[:, b], ph[0][:, b], ALU.subtract).then_inc(p_lo, 1)
                g = tile_of(i, 4)
                if g is not None:
                    for b in range(GB):
                        pool.wait_ge(s_hi, GB * g + b + 1)
                        if g >= 1:
                            pool.wait_ge(spv_done, g)
                        pool.tensor_tensor(sh[1][:, b], s32[:, b], sh[0][:, b], ALU.subtract).then_inc(s_lo, 1)
                if 2 <= i + 1 < TILES:
                    context_hi(i + 1)
                    context_lo(i + 1)
                g = tile_of(i, 2)
                if g is not None:
                    pool.wait_ge(ss_ready, g + 1)
                    if g >= 2:
                        pool.wait_ge(unit_ready, g - 1)
                    pool.wait_ge(guess_ready, g + 1)
                    pool.tensor_tensor(newton[:, :], guess[:, :], guess[:, :], ALU.mult).then_inc(newton_step, 1)
                    pool.wait_ge(newton_step, 3 * g + 1)
                    pool.tensor_tensor(newton[:, :], newton[:, :], ssm[:, :], ALU.mult).then_inc(newton_step, 1)
                    pool.wait_ge(newton_step, 3 * g + 2)
                    pool.tensor_scalar(newton[:, :], newton[:, :], -0.5, 1.5, ALU.mult, ALU.add
                                       ).then_inc(newton_step, 1)
                    pool.wait_ge(newton_step, 3 * g + 3)
                    pool.tensor_tensor(rnorm[:, g % 2, :], newton[:, :], guess[:, :], ALU.mult
                                       ).then_inc(rnorm_ready, 1)
                g = tile_of(i, 4)
                if g is not None:
                    inverse_std(2, g, g + 1, g + 1)
                g = tile_of(i, 1)
                if g is not None:
                    inverse_std(1, g, g + 1, g + 1)
                if i in (SLOTS - 3, SLOTS - 2):
                    chunk_hi(i - (SLOTS - 3))
            for c in range(2, CHUNKS):
                chunk_hi(c)

        @block.scalar
        def _(act):
            def keys_hi(g):
                for m in range(XP):
                    act.wait_ge(k_done, XP * g + m + 1)
                    act.copy(kt[0][:, m, :], bank(m)).then_inc(k_hi, 1)

            def values_hi(g):
                for n in range(2):
                    act.wait_ge(v_done, (GK // P) * g + 2 * n + 2)
                    act.copy(vx[0][:, g % 2, 2 * n:2 * n + 2, :, 0:XD],
                             bank(3 - n).rearrange("p (t h d) -> p t h d", t=2, h=XH)).then_inc(v_hi, 1)

            act.preload_act_table_set("natural_log_exp_and_others")
            for n in (1, 2, 0):
                act.wait_ge(d_wx[n], 16)
                act.copy(wx[0][:, n], wx_raw[:, n]).then_inc(wx_hi, 1)
            keys_hi(0)
            values_hi(0)
            for n in range(TILES // 2):
                act.wait_ge(ln1_turned, 2 * (n + 1))
                act.copy(lnt[0][:, :, n * 2 * P:(n + 1) * 2 * P].rearrange("p c (t m) -> p t c m", t=2),
                         bank(4 + n).rearrange("p (t c m) -> p t c m", t=2, c=KC)).then_inc(ln1_hi, 1)
            act.wait_ge(zeroed, 1)
            act.wait_ge(const_ready, 3)
            for half in range(2):
                for m in range(XP):
                    act.wait_ge(q_done, 2 * half + m + 1)
                    src = bank(2 * half + m).rearrange("p (b q) -> p b q", q=SEQ)
                    for j in range(2):
                        rows = slice(j * XD, (j + 1) * XD)
                        act.activation(qbd[0][rows, m, half * 8:half * 8 + 8, j * SEQ:(j + 1) * SEQ], src[rows],
                                       ACT.Copy, scale=XSCALE).then_inc(q_hi, 1)

            for i in range(SLOTS):
                g = tile_of(i, 1)
                if g is not None:
                    for b in range(GB):
                        act.wait_ge(negmax_ready, GB * g + b + 1)
                        if g >= 1:
                            act.wait_ge(p_lo, GB * (g - 1) + b + 1)
                        for m in range(XP):
                            ins = act.activation(p32[:, b, m], bank(4 + b)[:, m * CTX:(m + 1) * CTX], ACT.Exp,
                                                 bias=negmax[:, g, b, m:m + 1])
                        ins.then_inc(exp_done, 1)
                if 1 <= i < TILES:
                    keys_hi(i)
                g = tile_of(i, 4)
                if g is not None:
                    for b in range(GB):
                        act.wait_ge(ss_done, GB * g + b + 1)
                        if g >= 1:
                            act.wait_ge(s_lo, GB * (g - 1) + b + 1)
                        act.activation(s32[:, b], bank(6 + b).rearrange("p (a q) -> p a q", q=SEQ), ACT.Exp,
                                       bias=g_shift[:, 0:1], scale=g_sb[:, 0:1]).then_inc(sexp_done, 1)
                if 1 <= i < TILES:
                    values_hi(i)
                g2, g3 = tile_of(i, 2), tile_of(i, 5)
                if g3 is not None:
                    act.wait_ge(ln3_turned, g3 + 1)
                if g2 is not None:
                    act.wait_ge(ln2_turned, g2 + 1)
                    act.copy(ln2t[0][:, :, :], bank(6)[:, D:2 * D].rearrange("p (c m) -> p c m", c=KC)
                             ).then_inc(ln2_hi, 1)
                if g3 is not None:
                    act.copy(lnt[0][:, :, g3 * P:(g3 + 1) * P], bank(6)[:, 0:D].rearrange("p (c m) -> p c m", c=KC)
                             ).then_inc(ln3_hi, 1)
                g = tile_of(i, 1)
                if g is not None:
                    for b in range(GB):
                        act.wait_ge(p_turned, GB * g + b + 1)
                        act.copy(pt[:, b].rearrange("p s c h q -> p (s c h q)"), bank(4 + b).bitcast(F16)
                                 ).then_inc(pt_ready, 1)
                g = tile_of(i, 3)
                if g is not None:
                    act.wait_ge(q_turned, g + 1)
                    act.copy(qt[:, :, :].rearrange("p a q -> p (a q)"), bank(7).bitcast(F16)
                             ).then_inc(qt_ready, 1)
                    act.wait_ge(k_turned, g + 1)
                    src = bank(1).bitcast(F16).rearrange("p (a b k) -> p a b k", a=SP_, b=GB)
                    for j in range(2):
                        rows = slice(j * 4 * SD, (j + 1) * 4 * SD)
                        act.copy(kbd[rows, :, :, j, :], src[rows]).then_inc(kbd_ready, 1)
                g = tile_of(i, 2)
                if g is not None:
                    act.wait_ge(qkv_done, 2 * g + 1)
                    if g >= 1:
                        act.wait_ge(unit_ready, g)
                        act.wait_ge(ss_sum, g)
                    act.activation(sq[:, :], bank(0), ACT.Square).then_inc(sq_ready, 1)
                    act.copy(raw[:, :], bank(0)).then_inc(raw_ready, 1)
                    act.wait_ge(qkv_done, 2 * g + 2)
                    if g == 0:
                        act.wait_ge(zeroed, 10)
                    for b in range(GB):
                        for j in range(2):
                            src = bank(6)[b * SEQ:(b + 1) * SEQ, 0:D].rearrange("p (a j d) -> p a j d", j=2, d=SD)
                            act.copy(vbd[0][j * SEQ:(j + 1) * SEQ, g % 3, b, :, j, 0:SD], src[:, :, j]
                                     ).then_inc(sv_hi, 1)
                    act.wait_ge(ss_ready, g + 1)
                    if g >= 1:
                        act.wait_ge(rnorm_ready, g)
                    act.activation(logs[:, :], ssm[:, :], ACT.Ln, scale=LOG_LIFT).then_inc(log_ready, 1)
                    act.wait_ge(log_ready, g + 1)
                    act.activation(guess[:, :], logs[:, :], ACT.Exp, scale=-0.5, bias=half_log[:, 0:1]
                                   ).then_inc(guess_ready, 1)

            for n in range(2):
                act.wait_ge(logits_done, n + 1)
                act.activation(et[:, n * HALF:(n + 1) * HALF], bank(4 + n)[0:NE, :], ACT.Exp,
                               bias=bias_neg[:, 0:1], scale=-1.0).then_inc(et_ready, 1)
            act.wait_ge(p_lo, GB * TILES)
            act.wait_ge(s_done, GB * TILES)
            for c in range(CHUNKS):
                for n in range(2):
                    act.wait_ge(gate_done, 2 * c + n + 1)
                    if c >= 1:
                        act.wait_ge(h_ready, 2 * (c - 1) + n + 1)
                    act.activation(sg[:, n], bank(n), ACT.Silu).then_inc(sg_ready, 1)
                for n in range(2):
                    act.wait_ge(h_ready, 2 * c + n + 1)
                    if c >= 2:
                        act.wait_ge(down_done, TILES * (c - 1))
                    act.copy(hh[0][:, c % 2, n * HALF:(n + 1) * HALF], h32[:, n]).then_inc(h_hi, 1)

        @block.vector
        def _(dve):
            count = {"stat": 0, "route": 0}

            def layernorm_stats(n, g):
                dve.bn_stats(stats[n][:, g, :], xs[:, g, :]).then_inc(stat_ready, 1)
                count["stat"] += 1
                dve.wait_ge(stat_ready, count["stat"])
                dve.bn_aggr(meanvar[n][:, g, :], stats[n][:, g, :]).then_inc(ln_stats[n], 1)

            def normalize(n, g, dst, ready):
                dve.wait_ge(rstd_ready[n], g + 1)
                dve.wait_ge(ln_stats[n], g + 1)
                dve.tensor_scalar(dst, xs[:, g, :], meanvar[n][:, g, 0:1], rstd[n][:, g:g + 1],
                                  ALU.subtract, ALU.mult).then_inc(ready, 1)

            def weights_lo(k, n):
                dve.wait_ge(wx_hi, k + 1)
                dve.tensor_tensor(wx[1][:, n], wx_raw[:, n], wx[0][:, n].bitcast(F32), ALU.subtract
                                  ).then_inc(wx_lo, 1)

            def keys_lo(g):
                for m in range(XP):
                    dve.wait_ge(k_hi, XP * g + m + 1)
                    dve.tensor_tensor(kt[1][:, m, :], bank(m), kt[0][:, m, :].bitcast(F32), ALU.subtract
                                      ).then_inc(k_lo, 1)

            def values_lo(g):
                for n in range(2):
                    dve.wait_ge(v_hi, 2 * g + n + 1)
                    view = (slice(None), g % 2, slice(2 * n, 2 * n + 2), slice(None), slice(0, XD))
                    dve.tensor_tensor(vx[1][view], bank(3 - n).rearrange("p (t h d) -> p t h d", t=2, h=XH),
                                      vx[0][view], ALU.subtract).then_inc(v_lo, 1)

            def context_lo(g):
                dve.wait_ge(cx_hi, g + 1)
                dve.tensor_tensor(cx[1][:, g % 2], ctx_raw[g % 2][:, :, :], cx[0][:, g % 2].bitcast(F32),
                                  ALU.subtract).then_inc(cx_lo, 1)

            def chunk_lo(c):
                dve.wait_ge(wf_hi, c + 1)
                if c >= WBUF:
                    dve.wait_ge(down_done, TILES * (c - WBUF + 1))
                dve.tensor_tensor(wf[1][c % WBUF], wf_raw[c % 2], wf[0][c % WBUF].bitcast(F32),
                                  ALU.subtract).then_inc(wf_lo, 1)

            def ln1_part(n):
                dve.wait_ge(ln1_hi, n + 1)
                cols = slice(n * 2 * P, (n + 1) * 2 * P)
                dve.tensor_tensor(lnt[1][:, :, cols].rearrange("p c (t m) -> p t c m", t=2),
                                  bank(4 + n).rearrange("p (t c m) -> p t c m", t=2, c=KC),
                                  lnt[0][:, :, cols].bitcast(F32).rearrange("p c (t m) -> p t c m", t=2),
                                  ALU.subtract).then_inc(ln1_lo, 1)

            dve.memset(minus_half[:, :], -0.5).then_inc(const_ready, 1)
            dve.memset(ones[:, :], 1.0).then_inc(const_ready, 1)
            dve.memset(qbd[0][:, :, :, :].bitcast(F32), 0.0).then_inc(const_ready, 1)
            dve.memset(half_log[:, :], HALF_LOG).then_inc(const_ready, 1)
            weights_lo(0, 1)
            context_lo(0)
            weights_lo(1, 2)
            for g in range(TILES):
                dve.wait_ge(d_x[g // (TILES // 2)], 16)
                layernorm_stats(0, g)
            keys_lo(0)
            weights_lo(2, 0)
            for g in range(2):
                normalize(0, g, xn1[:, g, :], xn1_ready)
            values_lo(0)
            for g in range(2, TILES):
                dve.wait_ge(ln1_turned, g - 1)
                normalize(0, g, xn1[:, g % 2, :], xn1_ready)
                if g % 2 == 1:
                    ln1_part(g // 2 - 1)
            ln1_part(TILES // 2 - 1)
            dve.wait_ge(d_const, 16 * 6)
            dve.tensor_scalar(g_shift[:, :], g_sb[:, :], -1.0, None, ALU.mult).then_inc(const_ready, 1)
            dve.tensor_scalar(bias_neg[:, :], bias_sb[:, :], -1.0, None, ALU.mult).then_inc(const_ready, 1)
            dve.wait_ge(const_ready, 6)
            dve.tensor_tensor(g_shift[:, :], g_shift[:, :], g_sb[:, :], ALU.min).then_inc(const_ready, 1)
            dve.wait_ge(const_ready, 7)
            dve.tensor_scalar(g_shift[:, :], g_shift[:, :], LIFT, None, ALU.add).then_inc(const_ready, 1)
            for half in range(2):
                for m in range(XP):
                    src = bank(2 * half + m).rearrange("p (b q) -> p b q", q=SEQ)
                    for j in range(2):
                        rows = slice(j * XD, (j + 1) * XD)
                        view = (rows, m, slice(half * 8, half * 8 + 8), slice(j * SEQ, (j + 1) * SEQ))
                        dve.wait_ge(q_hi, 4 * half + 2 * m + j + 1)
                        dve.scalar_tensor_tensor(out=qbd[1][view], in0=src[rows], scalar=XSCALE,
                                                 in1=qbd[0][view].bitcast(F32), op0=ALU.mult, op1=ALU.subtract
                                                 ).then_inc(q_lo, 1)
            dve.wait_ge(ws_hi, 1)
            dve.tensor_tensor(ws[1][:, :, :], ws_raw[:, :, :], ws[0][:, :, :].bitcast(F32), ALU.subtract
                              ).then_inc(ws_lo, 1)
            dve.wait_ge(zeroed, 8)
            dve.tensor_copy(gate_hl[0][:, :, 0:NE], gate_raw[:, :, :]).then_inc(const_ready, 1)
            dve.wait_ge(const_ready, 9)
            dve.tensor_tensor(gate_hl[1][:, :, 0:NE], gate_raw[:, :, :], gate_hl[0][:, :, 0:NE].bitcast(F32),
                              ALU.subtract).then_inc(const_ready, 1)

            def add_attention(g, psum, heads, hd, rs, scaled, rs_ready, scaled_ready, x_done):
                dve.reciprocal(rs[:, g, :], psum[:, :, hd]).then_inc(rs_ready, 1)
                dve.wait_ge(rs_ready, g + 1)
                if g >= 1:
                    dve.wait_ge(x_done, g)
                dve.tensor_tensor(scaled[:, :].rearrange("p (h d) -> p h d", h=heads), psum[:, :, 0:hd],
                                  rs[:, g, :].unsqueeze(2).to_broadcast([P, heads, hd]), ALU.mult
                                  ).then_inc(scaled_ready, 1)
                dve.wait_ge(scaled_ready, g + 1)
                dve.tensor_tensor(xs[:, g, :], xs[:, g, :], scaled[:, :], ALU.add).then_inc(x_done, 1)
                dve.wait_ge(x_done, g + 1)

            for i in range(SLOTS):
                g = tile_of(i, 1)
                if g is not None:
                    for b in range(GB):
                        dve.wait_ge(s_done, GB * g + b + 1)
                        dve.tensor_reduce(negmax[:, g, b, :], bank(4 + b).rearrange("p (m k) -> p m k", m=XP),
                                          AX.X, ALU.max, negate=True).then_inc(negmax_ready, 1)
                g = tile_of(i, 3)
                if g is not None:
                    dve.wait_ge(rnorm_ready, g + 1)
                    dve.wait_ge(raw_ready, g + 1)
                    if g >= 1:
                        dve.wait_ge(stack_ready, 2 * g)
                    dve.tensor_tensor(unit[:, :, :, :].rearrange("p a h d -> p (a h) d"),
                                      raw[:, :].rearrange("p (h d) -> p h d", d=SD),
                                      rnorm[:, g % 2, :].unsqueeze(2).to_broadcast([P, 2 * SH, SD]), ALU.mult
                                      ).then_inc(unit_ready, 1)
                g = tile_of(i, 1)
                if g is not None:
                    for b in range(GB):
                        dve.wait_ge(exp_done, GB * g + b + 1)
                        if g >= 1:
                            dve.wait_ge(p_turned, GB * g)
                        dve.tensor_copy(ph[0][:, b], p32[:, b]).then_inc(p_hi, 1)
                g = tile_of(i, 2)
                if g is not None:
                    if g >= 1:
                        dve.wait_ge(ln2_turned, g)
                    normalize(1, g, xn2[:, :], xn2_ready)
                g = tile_of(i, 5)
                if g is not None:
                    if g >= 1:
                        dve.wait_ge(ln3_turned, g)
                    normalize(2, g, xn3[:, :], xn3_ready)
                if 1 <= i < TILES:
                    keys_lo(i)
                g = tile_of(i, 3)
                if g is not None:
                    twice = [unit[:, a].unsqueeze(2).to_broadcast([P, SH, 2, SD]) for a in range(2)]
                    views = [stack[a][:, :, :, :].rearrange("p h (u w) d -> p h u w d", u=2) for a in range(2)]
                    his = [views[0][:, :, :, 0, :], views[1][:, :, 0, :, :]]
                    los = [views[0][:, :, :, 1, :], views[1][:, :, 1, :, :]]
                    dve.wait_ge(unit_ready, g + 1)
                    if g >= 1:
                        dve.wait_ge(k_turned, g)
                    for a in range(2):
                        dve.tensor_copy(his[a], twice[a]).then_inc(stack_hi, 1)
                    for a in range(2):
                        dve.wait_ge(stack_hi, 2 * g + a + 1)
                        dve.tensor_tensor(los[a], twice[a], his[a], ALU.subtract).then_inc(stack_ready, 1)
                g = tile_of(i, 2)
                if g is not None:
                    dve.wait_ge(ln2_hi, g + 1)
                    if tile_of(i, 5) is not None:
                        dve.wait_ge(ln3_hi, tile_of(i, 5) + 1)
                    dve.tensor_tensor(ln2t[1][:, :, :], bank(6)[:, D:2 * D].rearrange("p (c m) -> p c m", c=KC),
                                      ln2t[0][:, :, :].bitcast(F32), ALU.subtract).then_inc(ln2_lo, 1)
                g = tile_of(i, 4)
                if g is not None:
                    for b in range(GB):
                        dve.wait_ge(sexp_done, GB * g + b + 1)
                        if g >= 1:
                            dve.wait_ge(spv_done, g)
                        dve.tensor_copy(sh[0][:, b], s32[:, b]).then_inc(s_hi, 1)
                g = tile_of(i, 5)
                if g is not None:
                    cols = slice(g * P, (g + 1) * P)
                    dve.wait_ge(ln3_hi, g + 1)
                    dve.tensor_tensor(lnt[1][:, :, cols], bank(6)[:, 0:D].rearrange("p (c m) -> p c m", c=KC),
                                      lnt[0][:, :, cols].bitcast(F32), ALU.subtract).then_inc(ln3_lo, 1)
                if 1 <= i < TILES:
                    values_lo(i)
                g = tile_of(i, 2)
                if g is not None:
                    dve.wait_ge(sq_ready, g + 1)
                    if g >= 1:
                        dve.wait_ge(ss_ready, g)
                    dve.tensor_reduce(ss[:, :], sq[:, :].rearrange("p (h d) -> p h d", d=SD), AX.X, ALU.add
                                      ).then_inc(ss_sum, 1)
                    dve.wait_ge(ss_sum, g + 1)
                    if g >= 1:
                        dve.wait_ge(rnorm_ready, g)
                    dve.tensor_scalar(ssm[:, :], ss[:, :], EPS_NORM ** 2, None, ALU.max).then_inc(ss_ready, 1)
                g = tile_of(i, 4)
                if g is not None:
                    dve.wait_ge(spv_done, g + 1)
                    add_attention(g, bank(3)[:, 0:SH * (SD + 1)].rearrange("p (h d) -> p h d", h=SH), SH, SD,
                                  rsum2, att2, rsum2_ready, att2_ready, x_self)
                    layernorm_stats(2, g)
                g = tile_of(i, 2)
                if g is not None:
                    dve.wait_ge(sv_hi, 4 * (g + 1))
                    for b in range(GB):
                        for j in range(2):
                            src = bank(6)[b * SEQ:(b + 1) * SEQ, 0:D].rearrange("p (a j d) -> p a j d", j=2, d=SD)
                            view = (slice(j * SEQ, (j + 1) * SEQ), g % 3, b, slice(None), j, slice(0, SD))
                            dve.tensor_tensor(vbd[1][view], src[:, :, j], vbd[0][view], ALU.subtract
                                              ).then_inc(sv_lo, 1)
                g = tile_of(i, 1)
                if g is not None:
                    dve.wait_ge(pv_done, g + 1)
                    add_attention(g, bank(2)[:, 0:XH * (XD + 1)].rearrange("p (h d) -> p h d", h=XH), XH, XD,
                                  rsum, att, rsum_ready, att_ready, x_cross)
                    layernorm_stats(1, g)
                if i in (SLOTS - 3, SLOTS - 2):
                    chunk_lo(i - (SLOTS - 3))

            def step(ins):
                ins.then_inc(route, 1)
                count["route"] += 1
                dve.wait_ge(route, count["route"])

            def over_experts(a):
                return a[:, :].unsqueeze(2).to_broadcast([P, TILES, NE])

            def over_tiles(a):
                return a[:, :].unsqueeze(1).to_broadcast([P, TILES, NE])

            def pick_first(src, best, hot):
                step(dve.tensor_reduce(best[:, :], src[:, :, :], AX.X, ALU.max))
                step(dve.tensor_tensor(r1[:, :, :], src[:, :, :], over_experts(best), ALU.is_equal))
                step(dve.tensor_tensor(r1[:, :, :], r1[:, :, :], rank_sb[:, :, :], ALU.mult))
                step(dve.tensor_reduce(pick[:, :], r1[:, :, :], AX.X, ALU.max))
                step(dve.tensor_tensor(hot[:, :, :], r1[:, :, :], over_experts(pick), ALU.is_equal))

            def gate_times_up(c):
                for n in range(2):
                    dve.wait_ge(sg_ready, 2 * c + n + 1)
                    dve.wait_ge(up_done, 2 * c + n + 1)
                    if c >= 1:
                        dve.wait_ge(h_hi, 2 * (c - 1) + n + 1)
                        dve.wait_ge(h_lo, 2 * (c - 1) + n + 1)
                    dve.tensor_tensor(h32[:, n], sg[:, n], bank(2 + n), ALU.mult).then_inc(h_ready, 1)
                for n in range(2):
                    dve.wait_ge(h_hi, 2 * c + n + 1)
                    dve.tensor_tensor(hh[1][:, c % 2, n * HALF:(n + 1) * HALF], h32[:, n],
                                      hh[0][:, c % 2, n * HALF:(n + 1) * HALF].bitcast(F32), ALU.subtract
                                      ).then_inc(h_lo, 1)

            def add_chunk(c):
                for t in range(TILES):
                    dve.wait_ge(down_done, TILES * c + 2 * (t // 2) + 2)
                    if c >= 1:
                        dve.wait_ge(x_ffn, TILES * (c - 1) + t + 1)
                    y = bank(4 + t // 2)[:, (t % 2) * D:(t % 2 + 1) * D]
                    if c < SHARED:
                        ins = dve.tensor_tensor(xs[:, t, :], y, xs[:, t, :], ALU.add)
                    else:
                        ins = dve.scalar_tensor_tensor(out=xs[:, t, :], in0=y,
                                                       scalar=coef[:, t, c - SHARED:c - SHARED + 1],
                                                       in1=xs[:, t, :], op0=ALU.mult, op1=ALU.add)
                    ins.then_inc(x_ffn, 1)

            dve.wait_ge(s_lo, GB * TILES)
            gate_times_up(0)
            dve.wait_ge(e_turned, TILES)
            step(dve.tensor_scalar(r1[:, :, :], bank(6)[:, 0:TILES * NE].rearrange("p (t e) -> p t e", t=TILES),
                                   1.0, None, ALU.add))
            step(dve.reciprocal(S[:, :, :], r1[:, :, :]))
            pick_first(S, top[0], onehot[0])
            step(dve.scalar_tensor_tensor(out=rest[:, :, :], in0=onehot[0][:, :, :], scalar=-2.0, in1=S[:, :, :],
                                          op0=ALU.mult, op1=ALU.add))
            pick_first(rest, top[1], onehot[1])
            step(dve.tensor_tensor(den[:, :], top[0][:, :], top[1][:, :], ALU.add))
            step(dve.tensor_scalar(den[:, :], den[:, :], 1e-8, None, ALU.add))
            step(dve.reciprocal(rden[:, :], den[:, :]))
            step(dve.tensor_tensor(tally[:, :, 1, :], onehot[0][:, :, :], onehot[1][:, :, :], ALU.add))
            step(dve.tensor_tensor(r1[:, :, :], S[:, :, :], tally[:, :, 1, :], ALU.mult))
            dve.tensor_tensor(tally[:, :, 0, :], r1[:, :, :], over_experts(rden), ALU.mult).then_inc(tally_ready, 1)
            gate_times_up(1)
            dve.wait_ge(tally_done, 1)
            step(dve.tensor_reduce(total[:, :], bank(7)[:, 0:TILES * 2 * NE].rearrange("p (t e) -> p e t", t=TILES),
                                   AX.X, ALU.add))
            step(dve.tensor_scalar(cnt[:, :], total[:, NE:], 1.0, None, ALU.max))
            step(dve.reciprocal(rcnt[:, :], cnt[:, :]))
            step(dve.tensor_tensor(wmean[:, :], total[:, 0:NE], rcnt[:, :], ALU.mult))
            step(dve.tensor_tensor(coef[:, :, :], tally[:, :, 1, :], over_tiles(wmean), ALU.mult))
            for c in range(CHUNKS):
                if c + 2 < CHUNKS:
                    chunk_lo(c + 2)
                if 2 <= c + 1 < CHUNKS:
                    gate_times_up(c + 1)
                add_chunk(c)

        @block.tensor
        def _(pe):
            def product(dst, lhs, rhs, k):
                n = 0
                for c in range(k):
                    for a, b in PARTS:
                        mm = pe.matmul(dst, lhs(a, c), rhs(b, c), start=(n == 0), stop=(n == 3 * k - 1))
                        n += 1
                return mm

            pe.wait_ge(d_const, 16 * 6)

            def keys(g):
                pe.wait_ge(cx_lo, g + 1)
                for m in range(XP):
                    product(bank(m), lambda a, c: wx[a][:, 1, c, m * P:(m + 1) * P],
                            lambda b, c: cx[b][:, g % 2, c, :], KC).then_inc(k_done, 1)

            def values(t, g):
                product(bank(3 - t // 2)[:, (t % 2) * D:(t % 2 + 1) * D],
                        lambda a, c: cx[a][:, g % 2, c, t * P:(t + 1) * P],
                        lambda b, c: wx[b][:, 2, c, :], KC).then_inc(v_done, 1)

            pe.wait_ge(wx_lo, 1)
            keys(0)
            pe.wait_ge(wx_lo, 2)
            for t in range(GK // P):
                values(t, 0)
            pe.wait_ge(d_const, 16 * 6)
            for t in range(TILES):
                pe.wait_ge(xn1_ready, t + 1)
                for c in range(KC):
                    o = ((t % 2) * KC + c) * P
                    mm = pe.transpose(bank(4 + t // 2)[:, o:o + P], xn1[:, t % 2, c * P:(c + 1) * P], id32[:, :])
                mm.then_inc(ln1_turned, 1)
            pe.wait_ge(wx_lo, 3)
            for half in range(2):
                pe.wait_ge(ln1_lo, 2 * (half + 1))
                pe.wait_ge(k_lo, XP) if half == 0 else pe.wait_ge(v_lo, 2)
                for m in range(XP):
                    product(bank(2 * half + m),
                            lambda a, c: wx[a][:, 0, c, m * P:(m + 1) * P],
                            lambda b, c: lnt[b][:, c, half * HALF:(half + 1) * HALF], KC).then_inc(q_done, 1)

            for i in range(1, SLOTS):
                g = tile_of(i, 1)
                if g is not None:
                    pe.wait_ge(k_lo, XP * (g + 1))
                    if g == 0:
                        pe.wait_ge(q_lo, 8)
                    for b in range(GB):
                        for m in range(XP):
                            mm = product(bank(4 + b)[:, m * CTX:(m + 1) * CTX],
                                         lambda a, c: qbd[a][:, m, GB * g + b, :],
                                         lambda r, c: kt[r][:, m, b * CTX:(b + 1) * CTX], 1)
                        mm.then_inc(s_done, 1)
                g = tile_of(i, 0)
                if g is not None:
                    if tile_of(i - 1, 2) is not None:
                        pe.wait_ge(raw_ready, tile_of(i - 1, 2) + 1)
                    if tile_of(i - 1, 3) is not None:
                        pe.wait_ge(kbd_ready, 2 * (tile_of(i - 1, 3) + 1))
                    keys(g)
                if tile_of(i - 1, 2) is not None:
                    pe.wait_ge(sv_lo, 4 * (tile_of(i - 1, 2) + 1))
                if tile_of(i - 1, 5) is not None:
                    pe.wait_ge(ln3_lo, tile_of(i - 1, 5) + 1)
                g = tile_of(i, 4)
                if g is not None:
                    pe.wait_ge(kbd_ready, 2 * (g + 1))
                    pe.wait_ge(qt_ready, g + 1)
                    for b in range(GB):
                        for a in range(SP_):
                            mm = pe.matmul(bank(6 + b)[:, a * SEQ:(a + 1) * SEQ], kbd[:, a, b, :, :],
                                           qt[:, a, b * SEQ:(b + 1) * SEQ], start=True, stop=True)
                        mm.then_inc(ss_done, 1)
                g = tile_of(i, 0)
                if g is not None:
                    if i == 1:
                        pe.wait_ge(q_lo, 8)
                    pe.wait_ge(v_lo, 2 * g)
                    for t in range(GK // P):
                        if t == 0 and tile_of(i - 1, 4) is not None:
                            pe.wait_ge(att2_ready, tile_of(i - 1, 4) + 1)
                        if t == 2 and tile_of(i - 1, 1) is not None:
                            pe.wait_ge(att_ready, tile_of(i - 1, 1) + 1)
                        values(t, g)
                if tile_of(i, 4) is not None:
                    pe.wait_ge(sexp_done, GB * (tile_of(i, 4) + 1))
                for lag, xn, xn_ready, half, turned in ((5, xn3, xn3_ready, 0, ln3_turned),
                                                        (2, xn2, xn2_ready, 1, ln2_turned)):
                    g = tile_of(i, lag)
                    if g is not None:
                        pe.wait_ge(xn_ready, g + 1)
                        for c in range(KC):
                            o = (half * KC + c) * P
                            mm = pe.transpose(bank(6)[:, o:o + P], xn[:, c * P:(c + 1) * P], id32[:, :])
                        mm.then_inc(turned, 1)
                g = tile_of(i, 1)
                if g is not None:
                    for b in range(GB):
                        pe.wait_ge(p_lo, GB * g + b + 1)
                        v = bank(4 + b).bitcast(F16)
                        for s in range(2):
                            for c in range(KC):
                                for m in range(XP):
                                    o = ((s * KC + c) * XP + m) * P
                                    mm = pe.transpose(v[:, o:o + P], ph[s][:, b, m, c * P:(c + 1) * P], id16[:, :])
                        mm.then_inc(p_turned, 1)
                g = tile_of(i, 3)
                if g is not None:
                    pe.wait_ge(k_lo, XP * (min(i, TILES - 1) + 1))
                    for n, (st, b, turned) in enumerate(((stack[0], 7, q_turned), (stack[1], 1, k_turned))):
                        pe.wait_ge(stack_ready, 2 * g + n + 1)
                        v = bank(b).bitcast(F16)
                        flat = st[:, :, :, :].rearrange("p h u d -> p (h u d)")
                        for a in range(SP_):
                            mm = pe.transpose(v[:, a * P:(a + 1) * P], flat[:, a * P:(a + 1) * P], id16[:, :])
                        mm.then_inc(turned, 1)
                g = tile_of(i, 2)
                if g is not None:
                    pe.wait_ge(ws_lo, 1)
                    pe.wait_ge(ln2_lo, g + 1)
                    pe.wait_ge(k_lo, XP * (min(i, TILES - 1) + 1))
                    if g >= 1:
                        pe.wait_ge(raw_ready, g)
                    for b, lo, hi in ((0, 0, 2 * D), (6, 2 * D, 3 * D)):
                        if b == 6 and tile_of(i, 5) is not None:
                            pe.wait_ge(ln3_lo, tile_of(i, 5) + 1)
                        product(bank(b)[:, 0:hi - lo], lambda a, c: ln2t[a][:, c, :],
                                lambda r, c: ws[r][:, c, lo:hi], KC).then_inc(qkv_done, 1)
                g = tile_of(i, 4)
                if g is not None:
                    pe.wait_ge(s_lo, GB * (g + 1))
                    pe.wait_ge(sv_lo, 4 * (g + 1))
                    if g >= 1:
                        pe.wait_ge(att2_ready, g)
                    if i < TILES:
                        pe.wait_ge(v_lo, 2 * i + 1)
                    for b in range(GB):
                        for a in range(SP_):
                            w = 2 * (SD + 1)
                            mm = product(bank(3)[b * SEQ:(b + 1) * SEQ, a * w:(a + 1) * w],
                                         lambda s, c: sh[s][:, b, a, :],
                                         lambda r, c: vbd[r][:, g % 3, b, a, :, :], 1)
                    mm.then_inc(spv_done, 1)
                g = tile_of(i, 1)
                if g is not None:
                    pe.wait_ge(pt_ready, GB * (g + 1))
                    pe.wait_ge(v_lo, 2 * (min(i, TILES - 1) + 1))
                    if g == 0:
                        pe.wait_ge(zeroed, 3)
                    else:
                        pe.wait_ge(att_ready, g)
                    for b in range(GB):
                        for h in range(XH):
                            mm = product(bank(2)[b * SEQ:(b + 1) * SEQ, h * (XD + 1):(h + 1) * (XD + 1)],
                                         lambda a, c: pt[:, b, a, c, h, :],
                                         lambda r, c: vx[r][:, g % 2, b * KC + c, h, :], KC)
                    mm.then_inc(pv_done, 1)

            pe.wait_ge(const_ready, 10)
            for n in range(2):
                pe.wait_ge(ln3_lo, (n + 1) * TILES // 2)
                product(bank(4 + n), lambda a, c: gate_hl[a][:, c, :],
                        lambda b, c: lnt[b][:, c, n * HALF:(n + 1) * HALF], KC).then_inc(logits_done, 1)

            def gate_and_up(c):
                pe.wait_ge(wf_lo, c + 1)
                for n in range(2):
                    for u, done in enumerate((gate_done, up_done)):
                        if c >= 1:
                            pe.wait_ge(sg_ready, 2 * (c - 1) + n + 1) if u == 0 else \
                                pe.wait_ge(h_ready, 2 * (c - 1) + n + 1)
                        product(bank(2 * u + n),
                                lambda a, k: wf[a][c % WBUF][:, (u * KC + k) * CH:(u * KC + k + 1) * CH],
                                lambda b, k: lnt[b][:, k, n * HALF:(n + 1) * HALF], KC).then_inc(done, 1)

            def down(c):
                pe.wait_ge(h_lo, 2 * (c + 1))
                for t in range(TILES):
                    if c >= 1:
                        pe.wait_ge(x_ffn, TILES * (c - 1) + 2 * (t // 2) + 2)
                    product(bank(4 + t // 2)[:, (t % 2) * D:(t % 2 + 1) * D],
                            lambda a, k: hh[a][:, c % 2, t * P:(t + 1) * P],
                            lambda b, k: wf[b][c % WBUF][:, 2 * KC * CH:], 1).then_inc(down_done, 1)

            gate_and_up(0)
            for t in range(TILES):
                pe.wait_ge(et_ready, t // (TILES // 2) + 1)
                pe.transpose(bank(6)[:, t * NE:(t + 1) * NE], et[:, t * P:(t + 1) * P], id32[0:NE, 0:NE]
                             ).then_inc(e_turned, 1)
            gate_and_up(1)
            pe.wait_ge(tally_ready, 1)
            pe.matmul(bank(7)[:, 0:TILES * 2 * NE], ones[:, :], tally[:, :, :, :], start=True, stop=True
                      ).then_inc(tally_done, 1)
            pe.wait_ge(et_ready, 2)
            pe.wait_ge(route, 1)
            for c in range(CHUNKS):
                if 2 <= c + 1 < CHUNKS:
                    gate_and_up(c + 1)
                if c == 0:
                    pe.wait_ge(route, ROUTE_TOTALS)
                down(c)


ROUTE_TOTALS = 2 + 5 + 1 + 5 + 5 + 1


def kernel(x, ctx_1024, L0_xattn_Wq, L0_xattn_Wk, L0_xattn_Wv, L0_attn_Wq, L0_attn_Wk, L0_attn_Wv,
           L0_attn_g_scale, L0_ffn_gate_w, L0_ffn_lb_bias, L0_ffn_expert_gate_w, L0_ffn_expert_up_w,
           L0_ffn_expert_down_w, L0_ffn_shared_gate_w, L0_ffn_shared_up_w, L0_ffn_shared_down_w):
    import numpy as np
    import concourse.bacc as bacc
    from concourse.bass_utils import run_bass_kernel_spmd

    def chunks(w):
        w = np.asarray(w)
        return w.T.reshape(w.shape[1] // P, P, w.shape[0]).transpose(1, 0, 2)

    def chunk_weights(gate, up, down):
        return np.concatenate([chunks(gate).reshape(P, -1), chunks(up).reshape(P, -1), np.asarray(down).T], axis=1)

    ctx_t = np.asarray(ctx_1024).reshape(TILES, GB, CTX, KC, P).transpose(0, 4, 3, 1, 2).reshape(TILES, P, KC, GK)
    sg, su, sd = (np.asarray(a) for a in (L0_ffn_shared_gate_w, L0_ffn_shared_up_w, L0_ffn_shared_down_w))
    eg, eu, ed = (np.asarray(a) for a in (L0_ffn_expert_gate_w, L0_ffn_expert_up_w, L0_ffn_expert_down_w))
    w_ffn = [chunk_weights(sg[n * CH:(n + 1) * CH], su[n * CH:(n + 1) * CH], sd[:, n * CH:(n + 1) * CH])
             for n in range(SHARED)]
    w_ffn += [chunk_weights(eg[n], eu[n], ed[n]) for n in range(NE)]
    arrays = {
        "x_tokens": np.asarray(x).reshape(TOK, D),
        "ctx_t": ctx_t,
        "w_cross": np.stack([chunks(w) for w in (L0_xattn_Wq, L0_xattn_Wk, L0_xattn_Wv)], axis=1),
        "w_self": np.concatenate([chunks(w) for w in (L0_attn_Wq, L0_attn_Wk, L0_attn_Wv)], axis=2),
        "g_scale": np.broadcast_to(np.asarray(L0_attn_g_scale).reshape(1, 1), (P, 1)),
        "gate_w": chunks(L0_ffn_gate_w),
        "lb_bias": np.asarray(L0_ffn_lb_bias).reshape(NE, 1),
        "w_ffn": np.stack(w_ffn),
        "ident32": np.eye(P, dtype=np.float32),
        "ident16": np.eye(P, dtype=np.float16),
        "rank": np.broadcast_to(np.arange(NE, 0, -1, dtype=np.float32), (P, TILES, NE)),
    }
    arrays = {k: np.ascontiguousarray(v) for k, v in arrays.items()}
    nc = bacc.Bacc("TRN2", target_bir_lowering=False, num_devices=1)
    args = [nc.dram_tensor(k, v.shape, mybir.dt.from_np(v.dtype), kind="ExternalInput").ap()
            for k, v in arrays.items()]
    out = nc.dram_tensor("out", (TOK, D), F32, kind="ExternalOutput").ap()
    build(nc, *args, out)
    r = run_bass_kernel_spmd(nc, [arrays], core_ids=[0])
    return r.results[0]["out"].reshape(BATCH, SEQ, D)
```

```python
from contextlib import ExitStack

import concourse.bass as bass
from concourse import mybir

ALU = mybir.AluOpType
ACT = mybir.ActivationFunctionType
AX = mybir.AxisListType
F32 = mybir.dt.float32
F32R = mybir.dt.float32r
F16 = mybir.dt.float16

P = 128
D = 256
KC = D // P
BATCH = 16
SEQ = 64
CTX = 256
TOK = BATCH * SEQ
TILES = TOK // P
GB = P // SEQ
GK = GB * CTX
XH = 4
XD = D // XH
XP = XH // 2
SH = 16
SD = D // SH
SP_ = SH // 2
NE = 8
CH = 128
WARM_UP = 18
WARM_WAIT = 6
SHARED = 2
CHUNKS = SHARED + NE
WC = 2 * KC * CH + D
WEIGHT_PIECES = (slice(0, 2 * KC * CH), slice(2 * KC * CH, WC))
WBUF = 4
SELF_LO_ON_DVE = TILES - 2
EARLY = WBUF
HALF = TOK // 2
ON_POOL = 2
ON_DVE = TILES - ON_POOL
EPS_LN = 1e-5
EPS_NORM = 1e-12
XSCALE = float(XD) ** -0.5
LOG_LIFT = 2.0 ** 20
HALF_LOG = 6.931471805599453
LIFT = 8.317766166719343

PARTS = ((0, 0), (0, 1), (1, 0))


def step_of(c, half):
    return EARLY * half + c if c < EARLY else 2 * c + half


STEPS = [(c, half) for half in range(2) for c in range(EARLY)] + \
        [(c, half) for c in range(EARLY, CHUNKS) for half in range(2)]


def gate_up_banks(k):
    if k < EARLY:
        return (4, 5) if k % 2 == 0 else (2, 0)
    return (1, 3) if k % 2 == 0 else (0, 2)


def dve_adds_before(c):
    return TILES + ON_DVE * (c - SHARED)


def downs_through(c):
    return TILES * max(c, SHARED - 1)


def build(nc, x, ctx_t, w_cross, w_self, g_scale, gate_w, lb_bias, w_ffn, ident32, ident16, rank, out):
    with ExitStack() as ctx:
        def sb(name, shape, dt=F32):
            return ctx.enter_context(nc.sbuf_tensor(name, shape, dt))

        def sem(name):
            return ctx.enter_context(nc.semaphore(name))

        id32 = sb("id32", [P, P])
        id16 = sb("id16", [P, P], F16)
        rank_sb = sb("rank_sb", [P, TILES, NE])
        ones = sb("ones", [P, P])
        minus_half = sb("minus_half", [P, 2 * SH])
        g_sb = sb("g_sb", [P, 1])
        g_shift = sb("g_shift", [P, 1])
        half_log = sb("half_log", [P, 1])
        bias_sb = sb("bias_sb", [NE, 1])
        bias_neg = sb("bias_neg", [NE, 1])
        gate_raw = sb("gate_raw", [P, KC, NE])
        gate_hl = [sb(f"gate_{n}", [P, KC, P], F32R) for n in ("hi", "lo")]
        xs = sb("xs", [P, TILES, D])
        wx_raw = sb("wx_raw", [P, 3, KC, D])
        wx = [sb(f"wx_{n}", [P, 3, KC, D], F32R) for n in ("hi", "lo")]
        ws_raw = sb("ws_raw", [P, KC, 3 * D])
        ws = [sb(f"ws_{n}", [P, KC, 3 * D], F32R) for n in ("hi", "lo")]
        stats = [sb(f"stats{n}", [P, TILES, 6]) for n in range(3)]
        meanvar = [sb(f"meanvar{n}", [P, TILES, 2]) for n in range(3)]
        veps = [sb(f"veps{n}", [P, TILES]) for n in range(3)]
        rstd = [sb(f"rstd{n}", [P, TILES]) for n in range(3)]
        xn1_own = sb("xn1", [P, 2, D])
        xn2 = sb("xn2", [P, D])
        xn3 = sb("xn3", [P, D])
        xn1 = [xn1_own[:, 0, :], xn1_own[:, 1, :], xn2[:, :], xn3[:, :]]
        lnt = [sb(f"lnt_{n}", [P, KC, TOK], F32R) for n in ("hi", "lo")]
        ln2t = [sb(f"ln2t_{n}", [P, KC, P], F32R) for n in ("hi", "lo")]
        ctx_raw = [sb(f"ctx_raw{n}", [P, KC, GK]) for n in range(2)]
        cx = [sb(f"cx_{n}", [P, 2, KC, GK], F32R) for n in ("hi", "lo")]
        qbd = [sb(f"qbd_{n}", [P, XP, BATCH, P], F32R) for n in ("hi", "lo")]
        kt = [sb(f"kt_{n}", [P, XP, GK], F32R) for n in ("hi", "lo")]
        vx = [sb(f"vx_{n}", [P, 2, GK // P, XH, XD + 1], F16) for n in ("hi", "lo")]
        negmax = sb("negmax", [P, TILES, GB, XP])
        p32 = sb("p32", [P, GB, XP, CTX])
        ph = [sb(f"p_{n}", [P, GB, XP, CTX], F16) for n in ("hi", "lo")]
        pt = sb("pt", [P, GB, 2, KC, XH, SEQ], F16)
        rsum = sb("rsum", [P, TILES, XH])
        att = sb("att", [P, D])
        raw = sb("raw", [P, 2 * D])
        sq = sb("sq", [P, 2 * D])
        ss = sb("ss", [P, 2 * SH])
        ssm = sb("ssm", [P, 2 * SH])
        logs = sb("logs", [P, 2 * SH])
        guess = sb("guess", [P, 2 * SH])
        newton = sb("newton", [P, 2 * SH])
        rnorm = sb("rnorm", [P, 2, 2 * SH])
        unit = sb("unit", [P, 2, SH, SD])
        stack = [sb(f"stack_{n}", [P, SH, 4, SD], F16) for n in ("q", "k")]
        qt = sb("qt", [P, SP_, P], F16)
        kbd = sb("kbd", [P, SP_, GB, 2, SEQ], F16)
        vbd = [sb(f"vbd_{n}", [P, 3, GB, SP_, 2, SD + 1], F16) for n in ("hi", "lo")]
        s32 = sb("s32", [P, GB, SP_, SEQ])
        sh = [sb(f"s_{n}", [P, GB, SP_, SEQ], F16) for n in ("hi", "lo")]
        rsum2 = sb("rsum2", [P, TILES, SH])
        att2 = sb("att2", [P, D])
        et = sb("et", [NE, TOK])
        S = sb("S", [P, TILES, NE])
        r1 = sb("r1", [P, TILES, NE])
        onehot = [sb(f"onehot{n}", [P, TILES, NE]) for n in range(2)]
        rest = sb("rest", [P, TILES, NE])
        top = [sb(f"top{n}", [P, TILES]) for n in range(2)]
        pick = sb("pick", [P, TILES])
        den = sb("den", [P, TILES])
        rden = sb("rden", [P, TILES])
        tally = sb("tally", [P, TILES, 2, NE])
        total = sb("total", [P, 2 * NE])
        cnt = sb("cnt", [P, NE])
        rcnt = sb("rcnt", [P, NE])
        wmean = sb("wmean", [P, NE])
        coef = sb("coef", [P, TILES, NE])
        wf_raw = [wx_raw[:, :, :, :].rearrange("p a c n -> p (a c n)")[:, n * WC:(n + 1) * WC] for n in range(2)]
        wf_own = [sb(f"wf_{n}", [P, 2, WC], F32R) for n in ("hi", "lo")]
        wf = [[wf_own[n][:, 0, :], wf_own[n][:, 1, :]]
              + [cx[n][:, u].rearrange("p c k -> p (c k)")[:, 0:WC] for u in range(2)] for n in range(2)]
        sg = p32[:, :, :, :].rearrange("p b m k -> p b (m k)")
        scaled_y = [att, att2]
        h32 = [sq[:, :], raw[:, :]]
        hh = [qbd[n][:, :, :, :].rearrange("p m b q -> p (m b q)").rearrange("p (u t) -> p u t", u=WBUF)
              for n in range(2)]

        ps = ctx.enter_context(nc.psum_tensor("ps", [P, 8, 512], F32))

        def bank(b):
            return ps[:, b, :]

        d_const, d_ident = sem("d_const"), sem("d_ident")
        d_x = [sem(f"d_x{n}") for n in range(2)]
        d_wx = [sem(f"d_wx{n}") for n in range(3)]
        d_ws = sem("d_ws")
        d_ctx = [sem(f"d_ctx{n}") for n in range(2)]
        d_wf = [sem(f"d_wf{n}") for n in range(2)]
        d_out = sem("d_out")
        zeroed, pairs_cleared = sem("zeroed"), sem("pairs_cleared")
        pool_veps = sem("pool_veps")
        rstd_ready = [sem(f"rstd{n}_ready") for n in range(3)]
        wx_hi, wx_lo = sem("wx_hi"), sem("wx_lo")
        ws_hi, ws_lo = sem("ws_hi"), sem("ws_lo")
        cx_hi, cx_lo = sem("cx_hi"), sem("cx_lo")
        wf_hi, wf_lo = sem("wf_hi"), sem("wf_lo")
        p_lo, s_lo, p_hi, s_hi = sem("p_lo"), sem("s_lo"), sem("p_hi"), sem("s_hi")
        newton_step, rnorm_ready = sem("newton_step"), sem("rnorm_ready")
        ln1_turned = sem("ln1_turned")
        q_done = sem("q_done")
        s_done, ss_done = sem("s_done"), sem("ss_done")
        k_done, v_done = sem("k_done"), sem("v_done")
        ln2_turned, ln3_turned = sem("ln2_turned"), sem("ln3_turned")
        p_turned, pv_done, spv_done = sem("p_turned"), sem("pv_done"), sem("spv_done")
        qkv_done = sem("qkv_done")
        q_turned, k_turned = sem("q_turned"), sem("k_turned")
        logits_done, e_turned, tally_done = sem("logits_done"), sem("e_turned"), sem("tally_done")
        gate_done, up_done, down_done = sem("gate_done"), sem("up_done"), sem("down_done")
        ln1_hi, q_hi = sem("ln1_hi"), sem("q_hi")
        exp_done, sexp_done = sem("exp_done"), sem("sexp_done")
        ln2_hi, ln3_hi = sem("ln2_hi"), sem("ln3_hi")
        first_cx_hi = sem("first_cx_hi")
        k_hi, v_hi, pt_ready = sem("k_hi"), sem("v_hi"), sem("pt_ready")
        raw_ready, sq_ready, sv_hi = sem("raw_ready"), sem("sq_ready"), sem("sv_hi")
        log_ready, guess_ready = sem("log_ready"), sem("guess_ready")
        kbd_ready, et_ready = sem("kbd_ready"), sem("et_ready")
        sg_ready, h_hi = sem("sg_ready"), sem("h_hi")
        const_ready = sem("const_ready")
        stat_ready = [sem(f"stat{n}_ready") for n in range(3)]
        ln_stats = [sem(f"ln{n}_stats") for n in range(3)]
        xn1_ready, xn2_ready, xn3_ready = sem("xn1_ready"), sem("xn2_ready"), sem("xn3_ready")
        ln1_lo, q_lo = sem("ln1_lo"), sem("q_lo")
        negmax_ready = sem("negmax_ready")
        unit_ready, stack_hi, stack_ready = sem("unit_ready"), sem("stack_hi"), sem("stack_ready")
        ln2_lo, ln3_lo = sem("ln2_lo"), sem("ln3_lo")
        k_lo, v_lo, sv_lo = sem("k_lo"), sem("v_lo"), sem("sv_lo")
        ss_sum, ss_ready = sem("ss_sum"), sem("ss_ready")
        rsum_ready, att_ready, x_cross = sem("rsum_ready"), sem("att_ready"), sem("x_cross")
        rsum2_ready, att2_ready, x_self = sem("rsum2_ready"), sem("att2_ready"), sem("x_self")
        qt_ready = sem("qt_ready")
        route = sem("route")
        tally_ready, coef_ready = sem("tally_ready"), sem("coef_ready")
        h_ready, h_lo, x_ffn = sem("h_ready"), sem("h_lo"), sem("x_ffn")
        y_scaled, x_pool = sem("y_scaled"), sem("x_pool")

        SLOTS = TILES + 5

        def tile_of(slot, lag):
            g = slot - lag
            return g if 0 <= g < TILES else None

        block = ctx.enter_context(nc.Block())

        @block.sync
        def _(sp):
            def load_x(n):
                h = TILES // 2
                sp.dma_start(xs[:, n * h:(n + 1) * h, :],
                             x.rearrange("(t p) d -> p t d", p=P)[:, n * h:(n + 1) * h, :]).then_inc(d_x[n], 16)

            load_x(0)
            sp.dma_start(ctx_raw[0][:, :, :], ctx_t[0]).then_inc(d_ctx[0], 16)
            for n in (1, 0):
                sp.dma_start(wx_raw[:, n], w_cross[:, n]).then_inc(d_wx[n], 16)
            sp.dma_start(id32[:, :], ident32).then_inc(d_ident, 16)
            sp.dma_start(wx_raw[:, 2], w_cross[:, 2]).then_inc(d_wx[2], 16)
            load_x(1)
            for dst, src in ((id16[:, :], ident16), (rank_sb[:, :, :], rank),
                             (g_sb[:, :], g_scale), (bias_sb[:, :], lb_bias), (gate_raw[:, :, :], gate_w)):
                sp.dma_start(dst, src).then_inc(d_const, 16)

            def load_chunk(c):
                if c == 0:
                    sp.wait_ge(wx_lo, 3)
                if c >= 2:
                    sp.wait_ge(wf_lo, 2 * (c - 1))
                sp.dma_start(wf_raw[c % 2], w_ffn[c]).then_inc(d_wf[c % 2], 16)

            for g in range(1, TILES):
                if g == 2:
                    sp.dma_start(ws_raw[:, :, :], w_self).then_inc(d_ws, 16)
                if g in (4, 5):
                    load_chunk(g - 4)
                if g >= 2:
                    sp.wait_ge(cx_lo, g - 1)
                sp.dma_start(ctx_raw[g % 2][:, :, :], ctx_t[g]).then_inc(d_ctx[g % 2], 16)
            for c in range(2, CHUNKS):
                load_chunk(c)
            for n in range(TILES // 2):
                if 2 * n >= ON_POOL:
                    sp.wait_ge(x_ffn, dve_adds_before(CHUNKS) - TILES + 2 * n + 2)
                else:
                    sp.wait_ge(x_pool, ON_POOL * NE)
                sp.dma_start(out.rearrange("(t p) d -> p t d", p=P)[:, 2 * n:2 * n + 2, :],
                             xs[:, 2 * n:2 * n + 2, :]).then_inc(d_out, 16)
            sp.wait_ge(d_out, 16 * (TILES // 2))

        @block.gpsimd
        def _(pool):
            def split_hi(dst, src):
                return pool.tensor_scalar(dst, src, 1.0, 0.0, ALU.mult, ALU.add)

            def inverse_std(n, g0, g1, stats_done):
                pool.wait_ge(ln_stats[n], stats_done)
                pool.tensor_scalar(veps[n][:, g0:g1], meanvar[n][:, g0:g1, 1], 1.0, EPS_LN, ALU.mult, ALU.add
                                   ).then_inc(pool_veps, 1)
                count["veps"] += 1
                pool.wait_ge(pool_veps, count["veps"])
                pool.tensor_tensor(rstd[n][:, g0:g1], veps[n][:, g0:g1], minus_half[:, 0:g1 - g0], ALU.pow
                                   ).then_inc(rstd_ready[n], g1 - g0)

            count = {"veps": 0}

            def context_hi(g):
                pool.wait_ge(d_ctx[g % 2], 16 * (g // 2 + 1))
                if g >= 2:
                    pool.wait_ge(v_done, (GK // P) * (g - 1))
                mine = slice(1, KC) if g == 0 else slice(0, KC)
                split_hi(cx[0][:, g % 2, mine], ctx_raw[g % 2][:, mine, :]).then_inc(cx_hi, 1)

            def context_lo(g):
                pool.wait_ge(cx_hi, g + 1)
                if g == 1:
                    pool.wait_ge(cx_lo, 1)
                pool.tensor_tensor(cx[1][:, g % 2], ctx_raw[g % 2][:, :, :], cx[0][:, g % 2].bitcast(F32),
                                   ALU.subtract).then_inc(cx_lo, 1)

            def chunk_hi(c, piece):
                if piece == 0:
                    pool.wait_ge(d_wf[c % 2], 16 * (c // 2 + 1))
                if c in (2, 3):
                    pool.wait_ge(v_done, (GK // P) * (TILES - 3 + c))
                if c >= WBUF:
                    pool.wait_ge(down_done, downs_through(c - WBUF)) if piece else \
                        pool.wait_ge(up_done, step_of(c - WBUF, 1) + 1)
                cols = WEIGHT_PIECES[piece]
                split_hi(wf[0][c % WBUF][:, cols], wf_raw[c % 2][:, cols]).then_inc(wf_hi, 1)

            def early_chunk(c, pieces):
                for piece in pieces:
                    cols = WEIGHT_PIECES[piece]
                    chunk_hi(c, piece)
                    pool.wait_ge(wf_hi, 2 * c + piece + 1)
                    pool.tensor_tensor(wf[1][c % WBUF][:, cols], wf_raw[c % 2][:, cols],
                                       wf[0][c % WBUF][:, cols].bitcast(F32), ALU.subtract).then_inc(wf_lo, 1)

            def early_hidden_lo(k):
                c, half = STEPS[k]
                tokens = slice(half * HALF, (half + 1) * HALF)
                pool.wait_ge(s_done, GB * TILES)
                pool.wait_ge(h_hi, k + 1)
                pool.tensor_tensor(hh[1][:, c % WBUF, tokens], h32[k % 2],
                                   hh[0][:, c % WBUF, tokens].bitcast(F32), ALU.subtract).then_inc(h_lo, 1)

            def clear_queries(n, half):
                b = BATCH // 2
                pool.memset(qbd[n][:, :, half * b:(half + 1) * b, :].bitcast(F32), 0.0).then_inc(zeroed, 1)

            clear_queries(1, 0)
            context_hi(0)
            pool.wait_ge(const_ready, 1)
            inverse_std(0, 0, TILES // 2, TILES // 2)
            pool.memset(vx[1][:, :, :, :, XD:], 0.0).then_inc(zeroed, 1)
            pool.memset(vx[0][:, :, :, :, XD:], 1.0).then_inc(zeroed, 1)
            context_hi(1)
            context_lo(1)
            for n in range(2):
                clear_queries(n, 1)
            for n in range(2):
                pool.memset(gate_hl[n][:, :, :].bitcast(F32), 0.0).then_inc(zeroed, 1)
            inverse_std(0, TILES // 2, TILES, TILES)

            for i in range(SLOTS):
                g = tile_of(i, 1)
                if g is not None:
                    for b in range(GB):
                        pool.wait_ge(p_hi, GB * g + b + 1)
                        if g >= 1:
                            pool.wait_ge(p_turned, GB * g)
                        pool.tensor_tensor(ph[1][:, b], p32[:, b], ph[0][:, b], ALU.subtract).then_inc(p_lo, 1)
                if i == 1:
                    pool.wait_ge(d_ws, 16)
                    split_hi(ws[0][:, :, :], ws_raw[:, :, :]).then_inc(ws_hi, 1)
                g = tile_of(i, 4)
                if g is not None and g < SELF_LO_ON_DVE:
                    for b in range(GB):
                        pool.wait_ge(s_hi, GB * g + b + 1)
                        if g >= 1:
                            pool.wait_ge(spv_done, g)
                        pool.tensor_tensor(sh[1][:, b], s32[:, b], sh[0][:, b], ALU.subtract).then_inc(s_lo, 1)
                if 2 <= i + 1 < TILES:
                    context_hi(i + 1)
                    context_lo(i + 1)
                if i == 1:
                    pool.memset(kbd[:, :, :, :, :].bitcast(F32), 0.0).then_inc(pairs_cleared, 1)
                    for n in range(2):
                        pool.memset(vbd[n][:, :, :, :, :, :], 0.0).then_inc(pairs_cleared, 1)
                    pool.wait_ge(pairs_cleared, 3)
                    for j in range(2):
                        rows = slice(j * SEQ, (j + 1) * SEQ)
                        pool.memset(vbd[0][rows, :, :, :, j, SD:], 1.0).then_inc(pairs_cleared, 1)
                        pool.wait_ge(pairs_cleared, 4 + j)
                if TILES - 1 <= i < TILES + 2:
                    early_chunk(i - (TILES - 1), (0, 1) if i <= TILES else (0,))
                g = tile_of(i, 2)
                if g is not None:
                    pool.wait_ge(ss_ready, g + 1)
                    if g >= 2:
                        pool.wait_ge(unit_ready, g - 1)
                    pool.wait_ge(guess_ready, g + 1)
                    pool.tensor_tensor(newton[:, :], guess[:, :], guess[:, :], ALU.mult).then_inc(newton_step, 1)
                    pool.wait_ge(newton_step, 3 * g + 1)
                    pool.tensor_tensor(newton[:, :], newton[:, :], ssm[:, :], ALU.mult).then_inc(newton_step, 1)
                    pool.wait_ge(newton_step, 3 * g + 2)
                    pool.tensor_scalar(newton[:, :], newton[:, :], -0.5, 1.5, ALU.mult, ALU.add
                                       ).then_inc(newton_step, 1)
                    pool.wait_ge(newton_step, 3 * g + 3)
                    pool.tensor_tensor(rnorm[:, g % 2, :], newton[:, :], guess[:, :], ALU.mult
                                       ).then_inc(rnorm_ready, 1)
                if i == TILES + 2:
                    early_hidden_lo(0)
                    early_hidden_lo(1)
                lags = ((1, tile_of(i, 1)), (2, tile_of(i, 4)))
                for n, g in lags:
                    if g is not None:
                        inverse_std(n, g, g + 1, g + 1)
                if i == TILES + 1:
                    early_chunk(2, (1,))
                    early_chunk(3, (0, 1))
            for k in range(2, EARLY + 2):
                early_hidden_lo(k)
            chunk_hi(EARLY, 0)
            early_hidden_lo(EARLY + 2)
            chunk_hi(EARLY, 1)
            early_hidden_lo(EARLY + 3)
            for c in range(SHARED, CHUNKS):
                if c + 3 < CHUNKS:
                    for piece in range(2):
                        chunk_hi(c + 3, piece)
                for t in range(ON_POOL):
                    n = ON_POOL * (c - SHARED) + t
                    pool.wait_ge(y_scaled, n + 1)
                    if c == SHARED:
                        pool.wait_ge(x_ffn, TILES)
                    else:
                        pool.wait_ge(x_pool, n - ON_POOL + 1)
                    pool.tensor_tensor(xs[:, t, :], xs[:, t, :], scaled_y[t][:, :], ALU.add).then_inc(x_pool, 1)

        @block.scalar
        def _(act):
            def keys_hi(g, pairs=range(XP)):
                for m in pairs:
                    act.wait_ge(k_done, XP * g + m + 1)
                    act.copy(kt[0][:, m, :], bank(m)).then_inc(k_hi, 1)

            def values_hi(g):
                for n in range(2):
                    act.wait_ge(v_done, (GK // P) * g + 2 * n + 2)
                    act.copy(vx[0][:, g % 2, 2 * n:2 * n + 2, :, 0:XD],
                             bank(2 + n).rearrange("p (t h d) -> p t h d", t=2, h=XH)).then_inc(v_hi, 1)

            def gate_activation(k):
                act.wait_ge(gate_done, k + 1)
                if k == 0:
                    act.wait_ge(p_lo, GB * TILES)
                if k >= 2:
                    act.wait_ge(h_ready, k - 1)
                act.activation(sg[:, k % 2], bank(gate_up_banks(k)[0]), ACT.Silu).then_inc(sg_ready, 1)

            def hidden_hi(k):
                c, half = STEPS[k]
                act.wait_ge(h_ready, k + 1)
                if c >= WBUF:
                    act.wait_ge(down_done, downs_through(c - WBUF))
                act.copy(hh[0][:, c % WBUF, half * HALF:(half + 1) * HALF], h32[k % 2]).then_inc(h_hi, 1)

            def router_exp(n):
                act.wait_ge(logits_done, n + 1)
                act.activation(et[:, n * HALF:(n + 1) * HALF], bank(ROUTER_BANKS[n])[0:NE, :], ACT.Exp,
                               bias=bias_neg[:, 0:1], scale=-1.0).then_inc(et_ready, 1)

            def ln1_hi_part(n):
                act.wait_ge(ln1_turned, 2 * (n + 1))
                act.copy(lnt[0][:, :, n * 2 * P:(n + 1) * 2 * P].rearrange("p c (t m) -> p t c m", t=2),
                         bank(4 + n).rearrange("p (t c m) -> p t c m", t=2, c=KC)).then_inc(ln1_hi, 1)

            def queries_hi(half):
                if half == 0:
                    act.wait_ge(const_ready, 3)
                act.wait_ge(zeroed, 5 if half else 1)
                for m in range(XP):
                    act.wait_ge(q_done, 2 * half + m + 1)
                    src = bank(6 + m).rearrange("p (b q) -> p b q", q=SEQ)
                    for j in range(2):
                        rows = slice(j * XD, (j + 1) * XD)
                        act.activation(qbd[0][rows, m, half * 8:half * 8 + 8, j * SEQ:(j + 1) * SEQ], src[rows],
                                       ACT.Copy, scale=XSCALE).then_inc(q_hi, 1)

            act.preload_act_table_set("natural_log_exp_and_others")
            act.wait_ge(d_ctx[0], 16)
            act.copy(cx[0][:, 0, 0], ctx_raw[0][:, 0, :]).then_inc(first_cx_hi, 1)
            for n in (1, 0, 2):
                act.wait_ge(d_wx[n], 16)
                act.copy(wx[0][:, n], wx_raw[:, n]).then_inc(wx_hi, 1)
            keys_hi(0, range(1))
            ln1_hi_part(0)
            ln1_hi_part(1)
            keys_hi(0, range(1, XP))
            queries_hi(0)

            for i in range(SLOTS):
                g = tile_of(i, 1)
                if g is not None:
                    for b in range(GB):
                        act.wait_ge(negmax_ready, GB * g + b + 1)
                        if g >= 1:
                            act.wait_ge(p_lo, GB * (g - 1) + b + 1)
                        for m in range(XP):
                            ins = act.activation(p32[:, b, m], bank(4 + b)[:, m * CTX:(m + 1) * CTX], ACT.Exp,
                                                 bias=negmax[:, g, b, m:m + 1])
                        ins.then_inc(exp_done, 1)
                if 1 <= i < TILES:
                    keys_hi(i)
                if i == TILES + 1:
                    gate_activation(0)
                    act.preload_act_table_set("natural_log_exp_and_others")
                g = tile_of(i, 4)
                if g is not None:
                    for b in range(GB):
                        act.wait_ge(ss_done, GB * g + b + 1)
                        if g >= 1:
                            act.wait_ge(s_lo, GB * (g - 1) + b + 1)
                        act.activation(s32[:, b], bank(6 + b).rearrange("p (a q) -> p a q", q=SEQ), ACT.Exp,
                                       bias=g_shift[:, 0:1], scale=g_sb[:, 0:1]).then_inc(sexp_done, 1)
                if i == TILES + 2:
                    gate_activation(1)
                if i == TILES + 3:
                    hidden_hi(0)
                    hidden_hi(1)
                    router_exp(0)
                    gate_activation(2)
                    gate_activation(3)
                if i == 1:
                    ln1_hi_part(2)
                    ln1_hi_part(3)
                if tile_of(i, 1) is not None:
                    values_hi(tile_of(i, 1))
                g2, g3 = tile_of(i, 2), tile_of(i, 5)
                if g3 is not None:
                    act.wait_ge(ln3_turned, g3 + 1)
                if g2 is not None:
                    act.wait_ge(ln2_turned, g2 + 1)
                    act.copy(ln2t[0][:, :, :], bank(6)[:, D:2 * D].rearrange("p (c m) -> p c m", c=KC)
                             ).then_inc(ln2_hi, 1)
                if g3 is not None:
                    act.copy(lnt[0][:, :, g3 * P:(g3 + 1) * P], bank(6)[:, 0:D].rearrange("p (c m) -> p c m", c=KC)
                             ).then_inc(ln3_hi, 1)
                g = tile_of(i, 1)
                if g is not None:
                    for b in range(GB):
                        act.wait_ge(p_turned, GB * g + b + 1)
                        act.copy(pt[:, b].rearrange("p s c h q -> p (s c h q)"), bank(4 + b).bitcast(F16)
                                 ).then_inc(pt_ready, 1)
                if i == 1:
                    queries_hi(1)
                g = tile_of(i, 3)
                if g is not None:
                    act.wait_ge(q_turned, g + 1)
                    act.copy(qt[:, :, :].rearrange("p a q -> p (a q)"), bank(7).bitcast(F16)
                             ).then_inc(qt_ready, 1)
                    act.wait_ge(k_turned, g + 1)
                    src = bank(1).bitcast(F16).rearrange("p (a b k) -> p a b k", a=SP_, b=GB)
                    for j in range(2):
                        rows = slice(j * 4 * SD, (j + 1) * 4 * SD)
                        act.copy(kbd[rows, :, :, j, :], src[rows]).then_inc(kbd_ready, 1)
                g = tile_of(i, 2)
                if g is not None:
                    act.wait_ge(qkv_done, 2 * g + 1)
                    if g >= 1:
                        act.wait_ge(unit_ready, g)
                        act.wait_ge(ss_sum, g)
                    act.activation(sq[:, :], bank(0), ACT.Square).then_inc(sq_ready, 1)
                    act.copy(raw[:, :], bank(0)).then_inc(raw_ready, 1)
                    act.wait_ge(qkv_done, 2 * g + 2)
                    if g == 0:
                        act.wait_ge(pairs_cleared, 5)
                    for b in range(GB):
                        for j in range(2):
                            src = bank(6)[b * SEQ:(b + 1) * SEQ, 0:D].rearrange("p (a j d) -> p a j d", j=2, d=SD)
                            act.copy(vbd[0][j * SEQ:(j + 1) * SEQ, g % 3, b, :, j, 0:SD], src[:, :, j]
                                     ).then_inc(sv_hi, 1)
                    act.wait_ge(ss_ready, g + 1)
                    if g >= 1:
                        act.wait_ge(rnorm_ready, g)
                    act.activation(logs[:, :], ssm[:, :], ACT.Ln, scale=LOG_LIFT).then_inc(log_ready, 1)
                    act.wait_ge(log_ready, g + 1)
                    act.activation(guess[:, :], logs[:, :], ACT.Exp, scale=-0.5, bias=half_log[:, 0:1]
                                   ).then_inc(guess_ready, 1)
                if i == TILES + 3:
                    hidden_hi(2)
                    hidden_hi(3)

            def scale_expert(c):
                if c == SHARED:
                    act.wait_ge(coef_ready, 1)
                if c > SHARED:
                    act.wait_ge(x_pool, ON_POOL * (c - SHARED))
                act.wait_ge(down_done, downs_through(c - 1) + ON_POOL)
                for t in range(ON_POOL):
                    act.activation(scaled_y[t][:, :], bank(4 + t // 2)[:, (t % 2) * D:(t % 2 + 1) * D], ACT.Copy,
                                   scale=coef[:, t, c - SHARED:c - SHARED + 1]).then_inc(y_scaled, 1)

            router_exp(1)
            for c in range(CHUNKS):
                if c < EARLY:
                    gate_activation(step_of(c, 1))
                    hidden_hi(step_of(c, 1))
                elif c < CHUNKS - 1:
                    for half in range(2):
                        gate_activation(step_of(c, half))
                    for half in range(2):
                        hidden_hi(step_of(c, half))
                    scale_expert(c - 2)
                else:
                    gate_activation(step_of(c, 0))
                    hidden_hi(step_of(c, 0))
                    scale_expert(c - 2)
                    gate_activation(step_of(c, 1))
                    hidden_hi(step_of(c, 1))
            for c in (CHUNKS - 2, CHUNKS - 1):
                scale_expert(c)

        @block.vector
        def _(dve):
            count = {"route": 0}

            def normalize(n, g, dst, ready):
                dve.wait_ge(rstd_ready[n], g + 1)
                dve.wait_ge(ln_stats[n], g + 1)
                dve.tensor_scalar(dst, xs[:, g, :], meanvar[n][:, g, 0:1], rstd[n][:, g:g + 1],
                                  ALU.subtract, ALU.mult).then_inc(ready, 1)

            def weights_lo(k, n):
                dve.wait_ge(wx_hi, k + 1)
                dve.tensor_tensor(wx[1][:, n], wx_raw[:, n], wx[0][:, n].bitcast(F32), ALU.subtract
                                  ).then_inc(wx_lo, 1)

            def keys_lo(g, pairs=range(XP)):
                for m in pairs:
                    dve.wait_ge(k_hi, XP * g + m + 1)
                    dve.tensor_tensor(kt[1][:, m, :], bank(m), kt[0][:, m, :].bitcast(F32), ALU.subtract
                                      ).then_inc(k_lo, 1)

            def values_lo(g):
                for n in range(2):
                    dve.wait_ge(v_hi, 2 * g + n + 1)
                    view = (slice(None), g % 2, slice(2 * n, 2 * n + 2), slice(None), slice(0, XD))
                    dve.tensor_tensor(vx[1][view], bank(2 + n).rearrange("p (t h d) -> p t h d", t=2, h=XH),
                                      vx[0][view], ALU.subtract).then_inc(v_lo, 1)

            def first_context_lo():
                for c in range(KC):
                    dve.wait_ge(cx_hi, 1) if c else dve.wait_ge(first_cx_hi, 1)
                    ins = dve.tensor_tensor(cx[1][:, 0, c], ctx_raw[0][:, c, :], cx[0][:, 0, c].bitcast(F32),
                                            ALU.subtract)
                ins.then_inc(cx_lo, 1)

            def chunk_lo(c, piece):
                dve.wait_ge(wf_hi, 2 * c + piece + 1)
                dve.wait_ge(wf_lo, 2 * c + piece)
                dve.wait_ge(down_done, downs_through(c - WBUF)) if piece else \
                    dve.wait_ge(up_done, step_of(c - WBUF, 1) + 1)
                cols = WEIGHT_PIECES[piece]
                dve.tensor_tensor(wf[1][c % WBUF][:, cols], wf_raw[c % 2][:, cols],
                                  wf[0][c % WBUF][:, cols].bitcast(F32), ALU.subtract).then_inc(wf_lo, 1)

            def ln1_part(n):
                dve.wait_ge(ln1_hi, n + 1)
                cols = slice(n * 2 * P, (n + 1) * 2 * P)
                dve.tensor_tensor(lnt[1][:, :, cols].rearrange("p c (t m) -> p t c m", t=2),
                                  bank(4 + n).rearrange("p (t c m) -> p t c m", t=2, c=KC),
                                  lnt[0][:, :, cols].bitcast(F32).rearrange("p c (t m) -> p t c m", t=2),
                                  ALU.subtract).then_inc(ln1_lo, 1)

            dve.memset(minus_half[:, :], -0.5).then_inc(const_ready, 1)
            dve.memset(ones[:, :], 1.0).then_inc(const_ready, 1)
            dve.memset(qbd[0][:, :, 0:BATCH // 2, :].bitcast(F32), 0.0).then_inc(const_ready, 1)
            dve.memset(half_log[:, :], HALF_LOG).then_inc(const_ready, 1)

            def stats_of_half(half):
                tiles = range(half * TILES // 2, (half + 1) * TILES // 2)
                dve.wait_ge(d_x[half], 16)
                for g in tiles:
                    dve.bn_stats(stats[0][:, g, :], xs[:, g, :]).then_inc(stat_ready[0], 1)
                dve.wait_ge(stat_ready[0], (half + 1) * TILES // 2)
                for g in tiles:
                    dve.bn_aggr(meanvar[0][:, g, :], stats[0][:, g, :]).then_inc(ln_stats[0], 1)

            def first_norm(g):
                if g >= 4:
                    dve.wait_ge(ln1_turned, g - 3)
                normalize(0, g, xn1[g % 4], xn1_ready)

            def queries_lo(half):
                for m in range(XP):
                    src = bank(6 + m).rearrange("p (b q) -> p b q", q=SEQ)
                    for j in range(2):
                        rows = slice(j * XD, (j + 1) * XD)
                        view = (rows, m, slice(half * 8, half * 8 + 8), slice(j * SEQ, (j + 1) * SEQ))
                        dve.wait_ge(q_hi, 4 * half + 2 * m + j + 1)
                        dve.scalar_tensor_tensor(out=qbd[1][view], in0=src[rows], scalar=XSCALE,
                                                 in1=qbd[0][view].bitcast(F32), op0=ALU.mult, op1=ALU.subtract
                                                 ).then_inc(q_lo, 1)

            stats_of_half(0)
            first_context_lo()
            weights_lo(0, 1)
            first_norm(0)
            first_norm(1)
            first_norm(2)
            first_norm(3)
            weights_lo(1, 0)
            ln1_part(0)
            ln1_part(1)
            keys_lo(0, range(1))
            weights_lo(2, 2)
            keys_lo(0, range(1, XP))
            queries_lo(0)
            stats_of_half(1)

            CROSS = (1, XH, XD, pv_done, rsum, rsum_ready, att, att_ready, x_cross)
            SELF = (2, SH, SD, spv_done, rsum2, rsum2_ready, att2, att2_ready, x_self)

            def row_sums(g, values, norm, heads, hd, done, rs, rs_ready, scaled, scaled_ready, x_done):
                dve.wait_ge(done, g + 1)
                dve.reciprocal(rs[:, g, :], values[:, :, hd]).then_inc(rs_ready, 1)

            def scale_values(g, values, norm, heads, hd, done, rs, rs_ready, scaled, scaled_ready, x_done):
                dve.wait_ge(rs_ready, g + 1)
                if g >= 1:
                    dve.wait_ge(x_done, g)
                dve.tensor_tensor(scaled[:, :].rearrange("p (h d) -> p h d", h=heads), values[:, :, 0:hd],
                                  rs[:, g, :].unsqueeze(2).to_broadcast([P, heads, hd]), ALU.mult
                                  ).then_inc(scaled_ready, 1)

            def add_values(g, values, norm, heads, hd, done, rs, rs_ready, scaled, scaled_ready, x_done):
                dve.wait_ge(scaled_ready, g + 1)
                dve.tensor_tensor(xs[:, g, :], xs[:, g, :], scaled[:, :], ALU.add).then_inc(x_done, 1)

            def first_stats(g, values, norm, heads, hd, done, rs, rs_ready, scaled, scaled_ready, x_done):
                dve.wait_ge(x_done, g + 1)
                dve.bn_stats(stats[norm][:, g, :], xs[:, g, :]).then_inc(stat_ready[norm], 1)

            def last_stats(g, values, norm, *rest):
                dve.wait_ge(stat_ready[norm], g + 1)
                dve.bn_aggr(meanvar[norm][:, g, :], stats[norm][:, g, :]).then_inc(ln_stats[norm], 1)

            def sum_of_squares(g):
                dve.wait_ge(sq_ready, g + 1)
                if g >= 1:
                    dve.wait_ge(ss_ready, g)
                dve.tensor_reduce(ss[:, :], sq[:, :].rearrange("p (h d) -> p h d", d=SD), AX.X, ALU.add
                                  ).then_inc(ss_sum, 1)

            def clamp_squares(g):
                dve.wait_ge(ss_sum, g + 1)
                if g >= 1:
                    dve.wait_ge(rnorm_ready, g)
                dve.tensor_scalar(ssm[:, :], ss[:, :], EPS_NORM ** 2, None, ALU.max).then_inc(ss_ready, 1)

            def self_value_lo(g, quarter):
                b, j = quarter // 2, quarter % 2
                if quarter == 0:
                    dve.wait_ge(sv_hi, 4 * (g + 1))
                src = bank(6)[b * SEQ:(b + 1) * SEQ, 0:D].rearrange("p (a j d) -> p a j d", j=2, d=SD)
                view = (slice(j * SEQ, (j + 1) * SEQ), g % 3, b, slice(None), j, slice(0, SD))
                dve.tensor_tensor(vbd[1][view], src[:, :, j], vbd[0][view], ALU.subtract).then_inc(sv_lo, 1)

            def unit_rows(g):
                dve.wait_ge(rnorm_ready, g + 1)
                dve.wait_ge(raw_ready, g + 1)
                if g >= 1:
                    dve.wait_ge(stack_ready, 2 * g)
                dve.tensor_tensor(unit[:, :, :, :].rearrange("p a h d -> p (a h) d"),
                                  raw[:, :].rearrange("p (h d) -> p h d", d=SD),
                                  rnorm[:, g % 2, :].unsqueeze(2).to_broadcast([P, 2 * SH, SD]), ALU.mult
                                  ).then_inc(unit_ready, 1)

            def negative_maxima(g, b):
                dve.wait_ge(s_done, GB * g + b + 1)
                dve.tensor_reduce(negmax[:, g, b, :], bank(4 + b).rearrange("p (m k) -> p m k", m=XP),
                                  AX.X, ALU.max, negate=True).then_inc(negmax_ready, 1)

            def self_probs_hi(g, b):
                dve.wait_ge(sexp_done, GB * g + b + 1)
                if g >= 1:
                    dve.wait_ge(spv_done, g)
                dve.tensor_copy(sh[0][:, b], s32[:, b]).then_inc(s_hi, 1)

            def self_probs_lo(g, b):
                dve.wait_ge(s_hi, GB * g + b + 1)
                dve.wait_ge(s_lo, GB * g + b)
                dve.tensor_tensor(sh[1][:, b], s32[:, b], sh[0][:, b], ALU.subtract).then_inc(s_lo, 1)

            def third_norm(g):
                if g is not None:
                    dve.wait_ge(ln3_turned, g) if g >= 1 else dve.wait_ge(ln1_turned, TILES)
                    normalize(2, g, xn3[:, :], xn3_ready)

            def third_norm_lo(g):
                if g is not None:
                    cols = slice(g * P, (g + 1) * P)
                    dve.wait_ge(ln3_hi, g + 1)
                    dve.tensor_tensor(lnt[1][:, :, cols], bank(6)[:, 0:D].rearrange("p (c m) -> p c m", c=KC),
                                      lnt[0][:, :, cols].bitcast(F32), ALU.subtract).then_inc(ln3_lo, 1)

            def hidden(k):
                dve.wait_ge(sg_ready, k + 1)
                dve.wait_ge(up_done, k + 1)
                if k == 0:
                    dve.wait_ge(ss_sum, TILES)
                if k == 1:
                    dve.wait_ge(unit_ready, TILES)
                if k >= 2:
                    dve.wait_ge(h_hi, k - 1)
                    dve.wait_ge(h_lo, k - 1)
                dve.tensor_tensor(h32[k % 2], sg[:, k % 2], bank(gate_up_banks(k)[1]), ALU.mult
                                  ).then_inc(h_ready, 1)

            def hidden_lo(k):
                c, half = STEPS[k]
                tokens = slice(half * HALF, (half + 1) * HALF)
                dve.wait_ge(h_hi, k + 1)
                if k == 2 * EARLY:
                    dve.wait_ge(h_lo, k)
                dve.tensor_tensor(hh[1][:, c % WBUF, tokens], h32[k % 2],
                                  hh[0][:, c % WBUF, tokens].bitcast(F32), ALU.subtract).then_inc(h_lo, 1)

            def add_shared(half):
                for t in range(half * TILES // 2, (half + 1) * TILES // 2):
                    dve.wait_ge(down_done, 2 * (t // 2) + 2)
                    y = bank(4 + t % 4 // 2)[:, (t % 2) * D:(t % 2 + 1) * D]
                    dve.tensor_tensor(xs[:, t, :], y, xs[:, t, :], ALU.add).then_inc(x_ffn, 1)

            def add_expert(c):
                for t in range(ON_POOL, TILES):
                    dve.wait_ge(down_done, downs_through(c - 1) + 2 * (t // 2) + 2)
                    dve.wait_ge(x_ffn, dve_adds_before(c) - TILES + t + 1 if c > SHARED else t + 1)
                    dve.scalar_tensor_tensor(out=xs[:, t, :], in0=bank(4 + t // 2)[:, (t % 2) * D:(t % 2 + 1) * D],
                                             scalar=coef[:, t, c - SHARED:c - SHARED + 1], in1=xs[:, t, :],
                                             op0=ALU.mult, op1=ALU.add).then_inc(x_ffn, 1)

            for i in range(SLOTS):
                rows, mine, cross, scores = tile_of(i, 3), tile_of(i, 5), tile_of(i, 2), tile_of(i, 1)

                def of_rows(step, *args):
                    if rows is not None:
                        step(rows, *args)

                def of_self(step, g=mine):
                    if g is not None:
                        step(g, bank(3)[:, 0:SH * (SD + 1)].rearrange("p (h d) -> p h d", h=SH), *SELF)

                def of_cross(step):
                    if cross is not None:
                        step(cross, bank(2)[:, 0:XH * (XD + 1)].rearrange("p (h d) -> p h d", h=XH), *CROSS)

                def of_scores(b):
                    if scores is not None:
                        negative_maxima(scores, b)

                of_rows(sum_of_squares)
                of_cross(row_sums)
                of_rows(clamp_squares)
                of_cross(scale_values)
                of_rows(self_value_lo, 0)
                of_cross(add_values)
                of_rows(self_value_lo, 1)
                of_cross(first_stats)
                of_rows(self_value_lo, 2)
                of_cross(last_stats)
                of_rows(self_value_lo, 3)
                if i < TILES + 3:
                    of_scores(0)
                    of_self(row_sums)
                    of_scores(1)
                    of_self(scale_values)
                    of_self(add_values)
                    if i == TILES + 2:
                        of_rows(unit_rows)
                    of_self(first_stats)
                elif i == TILES + 3:
                    last = tile_of(i, 4)
                    self_probs_hi(last, 0)
                    of_self(row_sums)
                    self_probs_lo(last, 0)
                    self_probs_hi(last, 1)
                    of_self(scale_values)
                    self_probs_lo(last, 1)
                    of_self(add_values)
                    of_self(first_stats)
                if TILES <= i < TILES + 4:
                    of_self(last_stats)
                if i > TILES:
                    if cross is not None:
                        dve.wait_ge(ln2_turned, cross)
                        normalize(1, cross, xn2[:, :], xn2_ready)
                if i != TILES + 2:
                    of_rows(unit_rows)
                if i < TILES:
                    of_self(last_stats)
                if i == 1:
                    first_norm(4)
                    first_norm(5)
                g = tile_of(i, 1)
                if g is not None:
                    for b in range(GB):
                        dve.wait_ge(exp_done, GB * g + b + 1)
                        if g >= 1:
                            dve.wait_ge(p_turned, GB * g)
                        dve.tensor_copy(ph[0][:, b], p32[:, b]).then_inc(p_hi, 1)
                g = tile_of(i, 2)
                if g is not None and i <= TILES:
                    dve.wait_ge(ln2_turned, g) if g >= 1 else dve.wait_ge(ln1_turned, TILES)
                    normalize(1, g, xn2[:, :], xn2_ready)
                if i == TILES + 3:
                    hidden(2)
                if i == TILES + 4:
                    hidden(3)
                if i != TILES + 2:
                    third_norm(tile_of(i, 5))
                if i == TILES + 3:
                    for part in (row_sums, scale_values, add_values, first_stats):
                        of_self(part, last)
                if i == 1:
                    first_norm(6)
                    first_norm(7)
                    ln1_part(2)
                    keys_lo(i, range(1))
                    ln1_part(3)
                    keys_lo(i, range(1, XP))
                elif 1 < i < TILES:
                    keys_lo(i)
                g = tile_of(i, 3)
                if g is not None:
                    twice = [unit[:, a].unsqueeze(2).to_broadcast([P, SH, 2, SD]) for a in range(2)]
                    views = [stack[a][:, :, :, :].rearrange("p h (u w) d -> p h u w d", u=2) for a in range(2)]
                    his = [views[0][:, :, :, 0, :], views[1][:, :, 0, :, :]]
                    los = [views[0][:, :, :, 1, :], views[1][:, :, 1, :, :]]
                    dve.wait_ge(unit_ready, g + 1)
                    if g >= 1:
                        dve.wait_ge(k_turned, g)
                    for a in range(2):
                        dve.tensor_copy(his[a], twice[a]).then_inc(stack_hi, 1)
                    if i == TILES + 2:
                        third_norm(tile_of(i, 5))
                    for a in range(2):
                        dve.wait_ge(stack_hi, 2 * g + a + 1)
                        dve.tensor_tensor(los[a], twice[a], his[a], ALU.subtract).then_inc(stack_ready, 1)
                g = tile_of(i, 2)
                if g is not None:
                    dve.wait_ge(ln2_hi, g + 1)
                    if tile_of(i, 5) is not None:
                        dve.wait_ge(ln3_hi, tile_of(i, 5) + 1)
                    dve.tensor_tensor(ln2t[1][:, :, :], bank(6)[:, D:2 * D].rearrange("p (c m) -> p c m", c=KC),
                                      ln2t[0][:, :, :].bitcast(F32), ALU.subtract).then_inc(ln2_lo, 1)
                if tile_of(i, 4) is not None and i < TILES + 3:
                    for b in range(GB):
                        self_probs_hi(tile_of(i, 4), b)
                    if i == TILES + 2:
                        for b in range(GB):
                            self_probs_lo(tile_of(i, 4), b)
                        hidden(0)
                third_norm_lo(tile_of(i, 5))
                if i == TILES + 3:
                    of_self(last_stats, last)
                if i == TILES + 2:
                    hidden(1)
                if tile_of(i, 1) is not None:
                    values_lo(tile_of(i, 1))
                if i == 1:
                    dve.wait_ge(ws_hi, 1)
                    dve.tensor_tensor(ws[1][:, :, :], ws_raw[:, :, :], ws[0][:, :, :].bitcast(F32), ALU.subtract
                                      ).then_inc(ws_lo, 1)
                    queries_lo(1)
                if i == 3:
                    dve.wait_ge(d_const, 16 * 5)
                    dve.tensor_scalar(g_shift[:, :], g_sb[:, :], -1.0, None, ALU.mult).then_inc(const_ready, 1)
                    dve.tensor_scalar(bias_neg[:, :], bias_sb[:, :], -1.0, None, ALU.mult).then_inc(const_ready, 1)
                    dve.wait_ge(const_ready, 6)
                    dve.tensor_tensor(g_shift[:, :], g_shift[:, :], g_sb[:, :], ALU.min).then_inc(const_ready, 1)
                    dve.wait_ge(const_ready, 7)
                    dve.tensor_scalar(g_shift[:, :], g_shift[:, :], LIFT, None, ALU.add).then_inc(const_ready, 1)
                    dve.wait_ge(zeroed, 7)
                    dve.tensor_copy(gate_hl[0][:, :, 0:NE], gate_raw[:, :, :]).then_inc(const_ready, 1)
                    dve.wait_ge(const_ready, 9)
                    dve.tensor_tensor(gate_hl[1][:, :, 0:NE], gate_raw[:, :, :], gate_hl[0][:, :, 0:NE].bitcast(F32),
                                      ALU.subtract).then_inc(const_ready, 1)

            def step(ins):
                ins.then_inc(route, 1)
                count["route"] += 1
                dve.wait_ge(route, count["route"])

            def over_experts(a):
                return a[:, :].unsqueeze(2).to_broadcast([P, TILES, NE])

            def over_tiles(a):
                return a[:, :].unsqueeze(1).to_broadcast([P, TILES, NE])

            def pick_first(src, best, hot):
                step(dve.tensor_reduce(best[:, :], src[:, :, :], AX.X, ALU.max))
                step(dve.tensor_tensor(r1[:, :, :], src[:, :, :], over_experts(best), ALU.is_equal))
                step(dve.tensor_tensor(r1[:, :, :], r1[:, :, :], rank_sb[:, :, :], ALU.mult))
                step(dve.tensor_reduce(pick[:, :], r1[:, :, :], AX.X, ALU.max))
                step(dve.tensor_tensor(hot[:, :, :], r1[:, :, :], over_experts(pick), ALU.is_equal))

            add_shared(0)
            hidden(4)
            hidden(5)
            dve.wait_ge(e_turned, TILES)
            step(dve.tensor_scalar(r1[:, :, :], bank(6)[:, 0:TILES * NE].rearrange("p (t e) -> p t e", t=TILES),
                                   1.0, None, ALU.add))
            step(dve.reciprocal(S[:, :, :], r1[:, :, :]))
            pick_first(S, top[0], onehot[0])
            hidden(6)
            step(dve.scalar_tensor_tensor(out=rest[:, :, :], in0=onehot[0][:, :, :], scalar=-2.0, in1=S[:, :, :],
                                          op0=ALU.mult, op1=ALU.add))
            pick_first(rest, top[1], onehot[1])
            chunk_lo(4, 0)
            hidden(7)
            step(dve.tensor_tensor(den[:, :], top[0][:, :], top[1][:, :], ALU.add))
            step(dve.tensor_scalar(den[:, :], den[:, :], 1e-8, None, ALU.add))
            step(dve.reciprocal(rden[:, :], den[:, :]))
            step(dve.tensor_tensor(tally[:, :, 1, :], onehot[0][:, :, :], onehot[1][:, :, :], ALU.add))
            step(dve.tensor_tensor(r1[:, :, :], S[:, :, :], tally[:, :, 1, :], ALU.mult))
            dve.tensor_tensor(tally[:, :, 0, :], r1[:, :, :], over_experts(rden), ALU.mult).then_inc(tally_ready, 1)
            add_shared(1)
            chunk_lo(4, 1)
            dve.wait_ge(tally_done, 1)
            step(dve.tensor_reduce(total[:, :], bank(7)[:, 0:TILES * 2 * NE].rearrange("p (t e) -> p e t", t=TILES),
                                   AX.X, ALU.add))
            step(dve.tensor_scalar(cnt[:, :], total[:, NE:], 1.0, None, ALU.max))
            step(dve.reciprocal(rcnt[:, :], cnt[:, :]))
            step(dve.tensor_tensor(wmean[:, :], total[:, 0:NE], rcnt[:, :], ALU.mult))
            dve.tensor_tensor(coef[:, :, :], tally[:, :, 1, :], over_tiles(wmean), ALU.mult).then_inc(coef_ready, 1)
            dve.wait_ge(coef_ready, 1)
            for c in range(SHARED, CHUNKS):
                if c + 3 < CHUNKS:
                    for piece in range(2):
                        chunk_lo(c + 3, piece)
                if c + 2 < CHUNKS - 1:
                    for half in range(2):
                        hidden(step_of(c + 2, half))
                    for half in range(2):
                        hidden_lo(step_of(c + 2, half))
                    add_expert(c)
                elif c + 2 < CHUNKS:
                    hidden(step_of(c + 2, 0))
                    hidden_lo(step_of(c + 2, 0))
                    add_expert(c)
                    hidden(step_of(c + 2, 1))
                    hidden_lo(step_of(c + 2, 1))
                else:
                    add_expert(c)

        @block.tensor
        def _(pe):
            def product(dst, lhs, rhs, k):
                n = 0
                for c in range(k):
                    for a, b in PARTS:
                        mm = pe.matmul(dst, lhs(a, c), rhs(b, c), start=(n == 0), stop=(n == 3 * k - 1))
                        n += 1
                return mm

            def key_pair(m, g):
                product(bank(m), lambda a, c: wx[a][:, 1, c, m * P:(m + 1) * P],
                        lambda b, c: cx[b][:, g % 2, c, :], KC).then_inc(k_done, 1)

            def keys(g):
                pe.wait_ge(cx_lo, g + 1)
                for m in range(XP):
                    key_pair(m, g)

            def values(t, g):
                product(bank(2 + t // 2)[:, (t % 2) * D:(t % 2 + 1) * D],
                        lambda a, c: cx[a][:, g % 2, c, t * P:(t + 1) * P],
                        lambda b, c: wx[b][:, 2, c, :], KC).then_inc(v_done, 1)

            def gate_or_up(k, u):
                c, half = STEPS[k]
                if u == 0:
                    pe.wait_ge(wf_lo, 2 * c + 1)
                if k == 0:
                    pe.wait_ge(ln3_lo, TILES // 2)
                if k == 1:
                    pe.wait_ge(att_ready, TILES) if u == 0 else pe.wait_ge(raw_ready, TILES)
                if k == EARLY:
                    pe.wait_ge(et_ready, 1) if u == 0 else pe.wait_ge(att2_ready, TILES)
                elif k == EARLY + 1:
                    pe.wait_ge(h_ready, EARLY)
                elif k >= 2:
                    pe.wait_ge(sg_ready, k - 1) if u == 0 else pe.wait_ge(h_ready, k - 1)
                product(bank(gate_up_banks(k)[u]),
                        lambda a, kc: wf[a][c % WBUF][:, (u * KC + kc) * CH:(u * KC + kc + 1) * CH],
                        lambda b, kc: lnt[b][:, kc, half * HALF:(half + 1) * HALF], KC
                        ).then_inc((gate_done, up_done)[u], 1)

            def gate_and_up(k):
                gate_or_up(k, 0)
                gate_or_up(k, 1)

            def logits(n):
                product(bank(ROUTER_BANKS[n]), lambda a, c: gate_hl[a][:, c, :],
                        lambda b, c: lnt[b][:, c, n * HALF:(n + 1) * HALF], KC).then_inc(logits_done, 1)

            def down_shared(half, tiles=range(TILES // 2)):
                pe.wait_ge(wf_lo, 2 * SHARED)
                pe.wait_ge(h_lo, step_of(SHARED - 1, half) + 1)
                if half == 0:
                    pe.wait_ge(h_ready, 3)
                else:
                    pe.wait_ge(x_ffn, TILES // 2)
                for t in (half * TILES // 2 + n for n in tiles):
                    product(bank(4 + t % 4 // 2)[:, (t % 2) * D:(t % 2 + 1) * D],
                            lambda a, c: hh[a][:, c, t * P:(t + 1) * P],
                            lambda b, c: wf[b][c][:, 2 * KC * CH:], SHARED).then_inc(down_done, 1)

            def down(c):
                pe.wait_ge(wf_lo, 2 * c + 2)
                pe.wait_ge(h_lo, step_of(c, 1) + 1)
                for t in range(TILES):
                    if c == SHARED:
                        pe.wait_ge(x_ffn, TILES)
                    elif t >= ON_POOL:
                        pe.wait_ge(x_ffn, dve_adds_before(c) - TILES + 2 * (t // 2) + 2)
                    else:
                        pe.wait_ge(y_scaled, ON_POOL * (c - SHARED))
                    product(bank(4 + t // 2)[:, (t % 2) * D:(t % 2 + 1) * D],
                            lambda a, k: hh[a][:, c % WBUF, t * P:(t + 1) * P],
                            lambda b, k: wf[b][c % WBUF][:, 2 * KC * CH:], 1).then_inc(down_done, 1)

            def turn_first_norm(g):
                pe.wait_ge(xn1_ready, g + 1)
                for c in range(KC):
                    o = ((g % 2) * KC + c) * P
                    mm = pe.transpose(bank(4 + g // 2)[:, o:o + P], xn1[g % 4][:, c * P:(c + 1) * P], id32[:, :])
                mm.then_inc(ln1_turned, 1)

            def queries(half):
                pe.wait_ge(ln1_lo, 2 * (half + 1))
                for m in range(XP):
                    product(bank(6 + m),
                            lambda a, c: wx[a][:, 0, c, m * P:(m + 1) * P],
                            lambda b, c: lnt[b][:, c, half * HALF:(half + 1) * HALF], KC).then_inc(q_done, 1)

            def keep_warm(b, n):
                for _ in range(n):
                    pe.matmul(bank(b)[:, 0:P], ones[:, :], ones[:, :], start=True, stop=True)

            pe.wait_ge(const_ready, 2)
            keep_warm(7, WARM_UP)
            pe.wait_ge(cx_lo, 1)
            pe.wait_ge(wx_lo, 1)
            key_pair(0, 0)
            pe.wait_ge(d_ident, 16)
            for g in range(TILES // 2):
                turn_first_norm(g)
            key_pair(1, 0)
            pe.wait_ge(wx_lo, 2)
            queries(0)
            pe.wait_ge(d_const, 16 * 5)

            def all_values(i, blocks):
                g = tile_of(i, 1)
                if g is None:
                    return
                if g == 0:
                    pe.wait_ge(wx_lo, 3)
                    pe.wait_ge(zeroed, 3)
                else:
                    pe.wait_ge(v_lo, 2 * g)
                for t in blocks:
                    if t == 0 and tile_of(i - 1, 1) is not None:
                        pe.wait_ge(att_ready, tile_of(i - 1, 1) + 1)
                    if t == 2 and tile_of(i - 1, 4) is not None:
                        pe.wait_ge(att2_ready, tile_of(i - 1, 4) + 1)
                    values(t, g)

            def self_scores(i):
                if tile_of(i - 1, 2) is not None:
                    pe.wait_ge(sv_lo, 4 * (tile_of(i - 1, 2) + 1))
                if tile_of(i - 1, 5) is not None:
                    pe.wait_ge(ln3_lo, tile_of(i - 1, 5) + 1)
                g = tile_of(i, 4)
                if g is None:
                    return
                pe.wait_ge(kbd_ready, 2 * (g + 1))
                pe.wait_ge(qt_ready, g + 1)
                for b in range(GB):
                    for a in range(SP_):
                        mm = pe.matmul(bank(6 + b)[:, a * SEQ:(a + 1) * SEQ], kbd[:, a, b, :, :],
                                       qt[:, a, b * SEQ:(b + 1) * SEQ], start=True, stop=True)
                    mm.then_inc(ss_done, 1)

            def self_values(i):
                g = tile_of(i, 4)
                if g is None:
                    return
                pe.wait_ge(s_lo, GB * (g + 1))
                pe.wait_ge(sv_lo, 4 * (g + 1))
                if g >= 1:
                    pe.wait_ge(att2_ready, g)
                if tile_of(i, 1) is not None:
                    pe.wait_ge(v_lo, 2 * (tile_of(i, 1) + 1))
                for b in range(GB):
                    for a in range(SP_):
                        w = 2 * (SD + 1)
                        mm = product(bank(3)[b * SEQ:(b + 1) * SEQ, a * w:(a + 1) * w],
                                     lambda s, c: sh[s][:, b, a, :],
                                     lambda r, c: vbd[r][:, g % 3, b, a, :, :], 1)
                mm.then_inc(spv_done, 1)

            for i in range(1, SLOTS):
                if i == 1:
                    all_values(i, range(GK // P))
                g = tile_of(i, 1)
                if g is not None:
                    pe.wait_ge(k_lo, XP * (g + 1))
                    if g in (0, TILES // 2):
                        pe.wait_ge(q_lo, 4 if g == 0 else 8)
                    for b in range(GB):
                        for m in range(XP):
                            mm = product(bank(4 + b)[:, m * CTX:(m + 1) * CTX],
                                         lambda a, c: qbd[a][:, m, GB * g + b, :],
                                         lambda r, c: kt[r][:, m, b * CTX:(b + 1) * CTX], 1)
                        mm.then_inc(s_done, 1)
                g = tile_of(i, 0)
                if g is not None:
                    if tile_of(i - 1, 2) is not None:
                        pe.wait_ge(raw_ready, tile_of(i - 1, 2) + 1)
                    if tile_of(i - 1, 3) is not None:
                        pe.wait_ge(kbd_ready, 2 * (tile_of(i - 1, 3) + 1))
                    keys(g)
                if i == 1:
                    for g in range(TILES // 2, TILES):
                        turn_first_norm(g)
                if i == TILES + 1:
                    gate_and_up(0)
                if i == TILES + 2:
                    gate_or_up(1, 1)
                if i != TILES:
                    self_scores(i)
                if i == TILES + 1:
                    gate_or_up(1, 0)
                if i == TILES + 2:
                    gate_or_up(2, 0)
                if i == TILES + 3:
                    pe.wait_ge(const_ready, 10)
                    logits(0)
                    gate_or_up(2, 1)
                    gate_or_up(3, 0)
                    self_values(i)
                if i >= 2:
                    all_values(i, range(GK // P // 2))
                if i == TILES:
                    self_scores(i)
                if i >= 2:
                    all_values(i, range(GK // P // 2, GK // P))
                if i == 2:
                    pe.wait_ge(q_lo, 8)
                if i == TILES + 2:
                    pe.wait_ge(att2_ready, TILES - 2)
                    keep_warm(3, WARM_WAIT)
                if tile_of(i, 4) is not None:
                    pe.wait_ge(sexp_done, GB * (tile_of(i, 4) + 1))
                for lag, xn, xn_ready, half, turned in ((5, xn3, xn3_ready, 0, ln3_turned),
                                                        (2, xn2, xn2_ready, 1, ln2_turned)):
                    g = tile_of(i, lag)
                    if g is not None:
                        pe.wait_ge(xn_ready, g + 1)
                        for c in range(KC):
                            o = (half * KC + c) * P
                            mm = pe.transpose(bank(6)[:, o:o + P], xn[:, c * P:(c + 1) * P], id32[:, :])
                        mm.then_inc(turned, 1)
                g = tile_of(i, 1)
                if g is not None:
                    for b in range(GB):
                        pe.wait_ge(p_lo, GB * g + b + 1)
                        v = bank(4 + b).bitcast(F16)
                        for s in range(2):
                            for c in range(KC):
                                for m in range(XP):
                                    o = ((s * KC + c) * XP + m) * P
                                    mm = pe.transpose(v[:, o:o + P], ph[s][:, b, m, c * P:(c + 1) * P], id16[:, :])
                        mm.then_inc(p_turned, 1)
                if i == 1:
                    queries(1)
                g = tile_of(i, 3)
                if g is not None:
                    for n, (st, b, turned) in enumerate(((stack[0], 7, q_turned), (stack[1], 1, k_turned))):
                        pe.wait_ge(stack_ready, 2 * g + n + 1)
                        if n == 1:
                            pe.wait_ge(k_lo, XP * (min(i, TILES - 1) + 1))
                        v = bank(b).bitcast(F16)
                        flat = st[:, :, :, :].rearrange("p h u d -> p (h u d)")
                        for a in range(SP_):
                            mm = pe.transpose(v[:, a * P:(a + 1) * P], flat[:, a * P:(a + 1) * P], id16[:, :])
                        mm.then_inc(turned, 1)
                g = tile_of(i, 2)
                if g is not None:
                    pe.wait_ge(ws_lo, 1)
                    pe.wait_ge(ln2_lo, g + 1)
                    pe.wait_ge(k_lo, XP * (min(i, TILES - 1) + 1))
                    if g >= 1:
                        pe.wait_ge(raw_ready, g)
                    for b, lo, hi in ((0, 0, 2 * D), (6, 2 * D, 3 * D)):
                        if b == 6 and tile_of(i, 5) is not None:
                            pe.wait_ge(ln3_lo, tile_of(i, 5) + 1)
                        product(bank(b)[:, 0:hi - lo], lambda a, c: ln2t[a][:, c, :],
                                lambda r, c: ws[r][:, c, lo:hi], KC).then_inc(qkv_done, 1)
                g = tile_of(i, 1)
                if g is not None:
                    pe.wait_ge(pt_ready, GB * (g + 1))
                    pe.wait_ge(v_lo, 2 * (g + 1))
                    if g >= 1:
                        pe.wait_ge(att_ready, g)
                    for b in range(GB):
                        for h in range(XH):
                            mm = product(bank(2)[b * SEQ:(b + 1) * SEQ, h * (XD + 1):(h + 1) * (XD + 1)],
                                         lambda a, c: pt[:, b, a, c, h, :],
                                         lambda r, c: vx[r][:, g % 2, b * KC + c, h, :], KC)
                    mm.then_inc(pv_done, 1)
                if i == TILES + 2:
                    keep_warm(3, WARM_WAIT)
                if i < TILES + 3:
                    self_values(i)
                if i == TILES + 3:
                    gate_or_up(3, 1)
                    down_shared(0, range(2))

            down_shared(0, range(2, TILES // 2))
            pe.wait_ge(ln3_lo, TILES)
            logits(1)
            gate_and_up(4)
            gate_and_up(5)
            pe.wait_ge(et_ready, 2)
            for t in range(TILES):
                pe.transpose(bank(6)[:, t * NE:(t + 1) * NE], et[:, t * P:(t + 1) * P], id32[0:NE, 0:NE]
                             ).then_inc(e_turned, 1)
            gate_and_up(6)
            down_shared(1)
            gate_and_up(7)
            for c in range(SHARED, CHUNKS):
                if c + 2 < CHUNKS:
                    for half in range(2 if c + 2 < CHUNKS - 1 else 1):
                        gate_and_up(step_of(c + 2, half))
                        if c == SHARED and half == 0:
                            pe.wait_ge(tally_ready, 1)
                            pe.matmul(bank(7)[:, 0:TILES * 2 * NE], ones[:, :], tally[:, :, :, :],
                                      start=True, stop=True).then_inc(tally_done, 1)
                if c == SHARED:
                    pe.wait_ge(route, ROUTE_TOTALS)
                down(c)
                if c + 2 == CHUNKS - 1:
                    gate_and_up(step_of(c + 2, 1))


ROUTER_BANKS = (1, 6)
ROUTE_TOTALS = 2 + 5 + 1 + 5 + 5 + 1


def kernel(x, ctx_1024, L0_xattn_Wq, L0_xattn_Wk, L0_xattn_Wv, L0_attn_Wq, L0_attn_Wk, L0_attn_Wv,
           L0_attn_g_scale, L0_ffn_gate_w, L0_ffn_lb_bias, L0_ffn_expert_gate_w, L0_ffn_expert_up_w,
           L0_ffn_expert_down_w, L0_ffn_shared_gate_w, L0_ffn_shared_up_w, L0_ffn_shared_down_w):
    import numpy as np
    import concourse.bacc as bacc
    from concourse.bass_utils import run_bass_kernel_spmd

    def chunks(w):
        w = np.asarray(w)
        return w.T.reshape(w.shape[1] // P, P, w.shape[0]).transpose(1, 0, 2)

    def chunk_weights(gate, up, down):
        return np.concatenate([chunks(gate).reshape(P, -1), chunks(up).reshape(P, -1), np.asarray(down).T], axis=1)

    ctx_t = np.asarray(ctx_1024).reshape(TILES, GB, CTX, KC, P).transpose(0, 4, 3, 1, 2).reshape(TILES, P, KC, GK)
    sg, su, sd = (np.asarray(a) for a in (L0_ffn_shared_gate_w, L0_ffn_shared_up_w, L0_ffn_shared_down_w))
    eg, eu, ed = (np.asarray(a) for a in (L0_ffn_expert_gate_w, L0_ffn_expert_up_w, L0_ffn_expert_down_w))
    w_ffn = [chunk_weights(sg[n * CH:(n + 1) * CH], su[n * CH:(n + 1) * CH], sd[:, n * CH:(n + 1) * CH])
             for n in range(SHARED)]
    w_ffn += [chunk_weights(eg[n], eu[n], ed[n]) for n in range(NE)]
    arrays = {
        "x_tokens": np.asarray(x).reshape(TOK, D),
        "ctx_t": ctx_t,
        "w_cross": np.stack([chunks(w) for w in (L0_xattn_Wq, L0_xattn_Wk, L0_xattn_Wv)], axis=1),
        "w_self": np.concatenate([chunks(w) for w in (L0_attn_Wq, L0_attn_Wk, L0_attn_Wv)], axis=2),
        "g_scale": np.broadcast_to(np.asarray(L0_attn_g_scale).reshape(1, 1), (P, 1)),
        "gate_w": chunks(L0_ffn_gate_w),
        "lb_bias": np.asarray(L0_ffn_lb_bias).reshape(NE, 1),
        "w_ffn": np.stack(w_ffn),
        "ident32": np.eye(P, dtype=np.float32),
        "ident16": np.eye(P, dtype=np.float16),
        "rank": np.broadcast_to(np.arange(NE, 0, -1, dtype=np.float32), (P, TILES, NE)),
    }
    arrays = {k: np.ascontiguousarray(v) for k, v in arrays.items()}
    nc = bacc.Bacc("TRN2", target_bir_lowering=False, num_devices=1)
    args = [nc.dram_tensor(k, v.shape, mybir.dt.from_np(v.dtype), kind="ExternalInput").ap()
            for k, v in arrays.items()]
    out = nc.dram_tensor("out", (TOK, D), F32, kind="ExternalOutput").ap()
    build(nc, *args, out)
    r = run_bass_kernel_spmd(nc, [arrays], core_ids=[0])
    return r.results[0]["out"].reshape(BATCH, SEQ, D)
```
